# Optimizing a Trainium2 kernel written in Bass

```python
import numpy as np
import jax
import jax.numpy as jnp

def _softmax(x, axis=-1):
    return jax.nn.softmax(x, axis=axis)

def _gelu(x):
    return jax.nn.gelu(x, approximate=True)

def _silu(x):
    return jax.nn.silu(x)

def _sigmoid(x):
    return jax.nn.sigmoid(x)

def _layernorm(x, axis=-1, eps=1e-05):
    m = jnp.mean(x, axis=axis, keepdims=True)
    v = jnp.var(x, axis=axis, keepdims=True)
    return (x - m) / jnp.sqrt(v + eps)

def _scatter_add(tgt, idx, src, axis=0):
    return tgt.at[idx].add(src)

def _segment_sum(src, seg, n):
    return jax.ops.segment_sum(src, seg, n)
kernel_name = 'mk_perceiver_d1_seqx_r2_8462a0'

def setup_inputs(seed: int=0):
    np.random.seed(seed)
    _w = jnp.asarray

    def _rec_inputs():
        import jax
        import jax.numpy as jnp
        _rk = jax.random.key(seed)
        x = -0.0002928 + 1 * jax.random.normal(jax.random.fold_in(_rk, 1), (8, 64, 512), jnp.float32)
        _lenS = 64 - jax.random.randint(jax.random.fold_in(_rk, 7), (8,), 0, max(1, 64 // 4) + 1, jnp.int32)
        _lenS2 = 1601 - jax.random.randint(jax.random.fold_in(_rk, 8), (8,), 0, max(1, 1601 // 4) + 1, jnp.int32)
        _ctx_1024P = jax.random.normal(jax.random.fold_in(_rk, 11), (8, 16, 512), jnp.float32)
        _ctx_1024c = jax.random.dirichlet(jax.random.fold_in(_rk, 511), 0.3 * jnp.ones((16,), jnp.float32), (8, 1601))
        _ctx_1024t = jnp.einsum('bsk,bkd->bsd', _ctx_1024c, _ctx_1024P)
        _ctx_1024t = _ctx_1024t * jax.lax.rsqrt(jnp.mean(jnp.square(_ctx_1024t)) + 1e-12) * 0.953939
        ctx_1024 = -1.39393e-06 + 0.999914 * (_ctx_1024t + 0.3 * jax.random.normal(jax.random.fold_in(_rk, 611), (8, 1601, 512), jnp.float32))
        _validS = jnp.arange(64)[None, :] < _lenS[:, None]
        _validS2 = jnp.arange(1601)[None, :] < _lenS2[:, None]
        _causal = jnp.tril(jnp.ones((64, 64), dtype=bool))
        mask_BxS2_bk1 = jnp.broadcast_to(_validS2[:, :], (8, 1601))
        return (x, ctx_1024, mask_BxS2_bk1)
    x, ctx_1024, mask_BxS2_bk1 = _rec_inputs()

    def _L0_xattn_setup():
        import jax, jax.numpy as jnp
        import numpy as np
        D_MODEL = 512
        N_HEADS = 16
        HEAD_DIM = D_MODEL // N_HEADS
        SCALE = HEAD_DIM ** (-0.5)
        MASK_FILL = -10000.0
        key = jax.random.key(seed)
        ks = jax.random.split(key, 12)
        B, L, D = (2, 1024, D_MODEL)
        inv = 1.0 / np.sqrt(D)
        inp = {'query': jax.random.normal(ks[0], (B, L, D), jnp.float32), 'key': jax.random.normal(ks[1], (B, L, D), jnp.float32), 'value': jax.random.normal(ks[2], (B, L, D), jnp.float32), 'Wq': jax.random.normal(ks[3], (D, D), jnp.float32) * inv, 'bq': jnp.zeros((D,), jnp.float32), 'Wk': jax.random.normal(ks[4], (D, D), jnp.float32) * inv, 'bk': jnp.zeros((D,), jnp.float32), 'Wv': jax.random.normal(ks[5], (D, D), jnp.float32) * inv, 'bv': jnp.zeros((D,), jnp.float32), 'Wo': jax.random.normal(ks[6], (D, D), jnp.float32) * inv, 'bo': jnp.zeros((D,), jnp.float32), 'valid_mask': jax.random.randint(ks[7], (B, L), 0, 2).astype(jnp.bool_)}
        return inp
    _L0_xattn_all = _L0_xattn_setup()
    _L0_xattn_in = {k: v for k, v in _L0_xattn_all.items() if k in ('Wq', 'bq', 'Wk', 'bk', 'Wv', 'bv', 'Wo', 'bo')}
    del _L0_xattn_all

    def _L0_attn_setup():
        import jax, jax.numpy as jnp
        import numpy as np
        NUM_HEADS = 16
        LAMBDA = 0.1
        HADAMARD_SCALE = 0.05
        ROPE_BASE = 10000.0

        def _rope(t):
            hd = t.shape[-1]
            S = t.shape[2]
            half = hd // 2
            inv_freq = 1.0 / ROPE_BASE ** (jnp.arange(half, dtype=jnp.float32) / half)
            ang = jnp.arange(S, dtype=jnp.float32)[:, None] * inv_freq[None, :]
            cos = jnp.cos(ang).astype(t.dtype)
            sin = jnp.sin(ang).astype(t.dtype)
            t1, t2 = (t[..., :half], t[..., half:])
            return jnp.concatenate([t1 * cos - t2 * sin, t2 * cos + t1 * sin], axis=-1)

        def _rotate_half(t):
            half = t.shape[-1] // 2
            return jnp.concatenate([-t[..., half:], t[..., :half]], axis=-1)
        key = jax.random.key(seed)
        ks = jax.random.split(key, 6)
        B, S, D = (2, 1024, 512)
        scale = 1.0 / np.sqrt(D).astype(np.float32)
        x = jax.random.normal(ks[0], (B, S, D), jnp.float32)
        Wq = jax.random.normal(ks[1], (D, D), jnp.float32) * scale
        Wk = jax.random.normal(ks[2], (D, D), jnp.float32) * scale
        Wv = jax.random.normal(ks[3], (D, D), jnp.float32) * scale
        Wo = jax.random.normal(ks[4], (D, D), jnp.float32) * scale
        gate_w = jax.random.normal(ks[5], (D // NUM_HEADS,), jnp.float32) * 0.01
        return {'x': x, 'Wq': Wq, 'Wk': Wk, 'Wv': Wv, 'Wo': Wo, 'gate_w': gate_w}
    _L0_attn_all = _L0_attn_setup()
    _L0_attn_in = {k: v for k, v in _L0_attn_all.items() if k in ('Wq', 'Wk', 'Wv', 'Wo', 'gate_w')}
    del _L0_attn_all

    def _L0_ffn_setup():
        import jax, jax.numpy as jnp
        import numpy as np
        D_MODEL = 512
        key = jax.random.key(seed)
        k_x, k_w, k_a1, k_a2 = jax.random.split(key, 4)
        x = jax.random.normal(k_x, (4, 1024, D_MODEL), dtype=jnp.float32)
        weight = jax.random.normal(k_w, (D_MODEL, D_MODEL), dtype=jnp.float32) * 0.02
        aux_weight1 = jax.random.normal(k_a1, (D_MODEL, D_MODEL), dtype=jnp.float32) * 0.02
        aux_weight2 = jax.random.normal(k_a2, (D_MODEL, D_MODEL), dtype=jnp.float32) * 0.02
        bias = jnp.zeros((D_MODEL,), dtype=jnp.float32)
        return {'x': x, 'weight': weight, 'aux_weight1': aux_weight1, 'aux_weight2': aux_weight2, 'bias': bias}
    _L0_ffn_all = _L0_ffn_setup()
    _L0_ffn_in = {k: v for k, v in _L0_ffn_all.items() if k in ('weight', 'aux_weight1', 'aux_weight2', 'bias')}
    del _L0_ffn_all
    return {'x': x, 'ctx_1024': ctx_1024, 'mask_BxS2_bk1': mask_BxS2_bk1, 'L0_xattn_Wq': _L0_xattn_in['Wq'], 'L0_xattn_bq': _L0_xattn_in['bq'], 'L0_xattn_Wk': _L0_xattn_in['Wk'], 'L0_xattn_bk': _L0_xattn_in['bk'], 'L0_xattn_Wv': _L0_xattn_in['Wv'], 'L0_xattn_bv': _L0_xattn_in['bv'], 'L0_xattn_Wo': _L0_xattn_in['Wo'], 'L0_xattn_bo': _L0_xattn_in['bo'], 'L0_attn_Wq': _L0_attn_in['Wq'], 'L0_attn_Wk': _L0_attn_in['Wk'], 'L0_attn_Wv': _L0_attn_in['Wv'], 'L0_attn_Wo': _L0_attn_in['Wo'], 'L0_attn_gate_w': _L0_attn_in['gate_w'], 'L0_ffn_weight': _L0_ffn_in['weight'], 'L0_ffn_aux_weight1': _L0_ffn_in['aux_weight1'], 'L0_ffn_aux_weight2': _L0_ffn_in['aux_weight2'], 'L0_ffn_bias': _L0_ffn_in['bias']}

def reference(x, ctx_1024, mask_BxS2_bk1, L0_xattn_Wq, L0_xattn_bq, L0_xattn_Wk, L0_xattn_bk, L0_xattn_Wv, L0_xattn_bv, L0_xattn_Wo, L0_xattn_bo, L0_attn_Wq, L0_attn_Wk, L0_attn_Wv, L0_attn_Wo, L0_attn_gate_w, L0_ffn_weight, L0_ffn_aux_weight1, L0_ffn_aux_weight2, L0_ffn_bias):
    import jax
    import jax.numpy as jnp

    def _L0_xattn_ref(query, key, value, Wq, bq, Wk, bk, Wv, bv, Wo, bo, valid_mask):
        import jax, jax.numpy as jnp
        import numpy as np
        D_MODEL = 512
        N_HEADS = 16
        HEAD_DIM = D_MODEL // N_HEADS
        SCALE = HEAD_DIM ** (-0.5)
        MASK_FILL = -10000.0
        B, Lq, D = query.shape
        Lk = key.shape[1]
        H, HD = (N_HEADS, HEAD_DIM)
        Q = (query @ Wq.T + bq).reshape(B, Lq, H, HD).transpose(0, 2, 1, 3)
        K = (key @ Wk.T + bk).reshape(B, Lk, H, HD).transpose(0, 2, 1, 3)
        V = (value @ Wv.T + bv).reshape(B, Lk, H, HD).transpose(0, 2, 1, 3)
        scores = jnp.einsum('bhqd,bhkd->bhqk', Q, K) * SCALE
        scores = jnp.where(valid_mask[:, None, None, :], scores, MASK_FILL)
        weights = jax.nn.softmax(scores, axis=-1)
        out = jnp.einsum('bhqk,bhkd->bhqd', weights, V)
        out = out.transpose(0, 2, 1, 3).reshape(B, Lq, D)
        out = out @ Wo.T + bo
        gate = jnp.any(valid_mask, axis=1).astype(out.dtype)[:, None, None]
        return out * gate

    def _L0_attn_ref(x, Wq, Wk, Wv, Wo, gate_w):
        import jax, jax.numpy as jnp
        import numpy as np
        NUM_HEADS = 16
        LAMBDA = 0.1
        HADAMARD_SCALE = 0.05
        ROPE_BASE = 10000.0

        def _rope(t):
            hd = t.shape[-1]
            S = t.shape[2]
            half = hd // 2
            inv_freq = 1.0 / ROPE_BASE ** (jnp.arange(half, dtype=jnp.float32) / half)
            ang = jnp.arange(S, dtype=jnp.float32)[:, None] * inv_freq[None, :]
            cos = jnp.cos(ang).astype(t.dtype)
            sin = jnp.sin(ang).astype(t.dtype)
            t1, t2 = (t[..., :half], t[..., half:])
            return jnp.concatenate([t1 * cos - t2 * sin, t2 * cos + t1 * sin], axis=-1)

        def _rotate_half(t):
            half = t.shape[-1] // 2
            return jnp.concatenate([-t[..., half:], t[..., :half]], axis=-1)
        B, S, D = x.shape
        H = NUM_HEADS
        hd = D // H

        def heads(W):
            return (x @ W.T).reshape(B, S, H, hd).transpose(0, 2, 1, 3)
        Q = _rope(heads(Wq))
        K = _rope(heads(Wk))
        V = heads(Wv)
        causal = jnp.tril(jnp.ones((S, S), dtype=bool))
        inv_sqrt_d = 1.0 / jnp.sqrt(jnp.asarray(hd, x.dtype))

        def attend(q, k):
            s = (jnp.einsum('bhsd,bhtd->bhst', q, k) + LAMBDA * jnp.einsum('bhsd,bhtd->bhst', q * q, k * k)) * inv_sqrt_d
            s = jnp.where(causal, s, jnp.asarray(-1000000000.0, s.dtype))
            a = jax.nn.softmax(s, axis=-1)
            return jnp.einsum('bhst,bhtd->bhsd', a, V)
        out1 = attend(Q, K)
        out2 = attend(_rotate_half(Q), _rotate_half(K))
        out = 0.5 * (out1 + out2) + HADAMARD_SCALE * (out1 * out2) * gate_w
        out = out.transpose(0, 2, 1, 3).reshape(B, S, D)
        return out @ Wo.T

    def _L0_ffn_ref(x, weight, aux_weight1, aux_weight2, bias):
        import jax, jax.numpy as jnp
        import numpy as np
        D_MODEL = 512
        h = jnp.einsum('btc,cd->btd', x, weight)
        h = jnp.einsum('btc,cd->btd', h, aux_weight1)
        h = jnp.einsum('btc,cd->btd', h, aux_weight2)
        return jnp.tanh(h + bias)
    x = x + _L0_xattn_ref(_layernorm(x, axis=-1), ctx_1024, ctx_1024, L0_xattn_Wq, L0_xattn_bq, L0_xattn_Wk, L0_xattn_bk, L0_xattn_Wv, L0_xattn_bv, L0_xattn_Wo, L0_xattn_bo, mask_BxS2_bk1)
    x = x + _L0_attn_ref(_layernorm(x, axis=-1), L0_attn_Wq, L0_attn_Wk, L0_attn_Wv, L0_attn_Wo, L0_attn_gate_w)
    x = x + _L0_ffn_ref(_layernorm(x, axis=-1), L0_ffn_weight, L0_ffn_aux_weight1, L0_ffn_aux_weight2, L0_ffn_bias)
    return x

_drawn_inputs = setup_inputs


def setup_inputs(seed=0):
    import zlib

    import numpy as np

    out = dict(_drawn_inputs(seed))
    spreads = {'L0_xattn_bq': (0.0, 0.346),
     'L0_xattn_bk': (0.0, 2.0),
     'L0_xattn_bv': (0.0, 0.1),
     'L0_xattn_bo': (0.0, 0.1),
     'L0_ffn_bias': (0.0, 0.1)}
    factors = {'L0_attn_gate_w': 200.0}
    for name, (base, spread) in spreads.items():
        noise = np.random.default_rng([zlib.crc32(name.encode()), seed]).standard_normal(out[name].shape)
        drawn = base * np.exp(spread * noise) if base else spread * noise
        out[name] = jnp.asarray(drawn.astype(out[name].dtype))
    for name, factor in factors.items():
        out[name] = (out[name] * factor).astype(out[name].dtype)
    return out
```

```python
from contextlib import ExitStack

import concourse.bass as bass
import numpy as np
from concourse import mybir

F32 = mybir.dt.float32
F32R = mybir.dt.float32r
BF16 = mybir.dt.bfloat16
F16 = mybir.dt.float16
U8 = mybir.dt.uint8
ALU = mybir.AluOpType
ACT = mybir.ActivationFunctionType
AX = mybir.AxisListType

P = 128
B, LQ, D = 8, 64, 512
S2, S2P = 1601, 1602
H, HD = 16, 32
KC = D // P
T = B * LQ
M = T // P
EPS = 1e-5
XSCALE = HD ** -0.5
FILL = -10000.0

CH = [(0, 384), (384, 384), (768, 384), (1152, 450)]
NT = -(-S2 // P)
ROWS = [min(P, S2 - P * t) for t in range(NT)]
CHUNK_END = [3, 6, 9, 13]
PAIRS = 4
VRING, PTRING = 8, 3

SLOTS = 20
T_LAG, PV_LAG = 5, 7
K_SLOT = {5: (0, 0), 6: (0, 1), 8: (1, 0), 10: (1, 1), 14: (2, 0), 15: (2, 1), 18: (3, 0), 19: (3, 1)}
XH_SLOT = {3: 0, 6: 1, 9: 2, 13: 3}
V_PIECE, K_PIECE = {}, {}
for _s in range(SLOTS):
    if _s < NT:
        V_PIECE[_s] = len(V_PIECE) + len(K_PIECE)
    if _s in K_SLOT:
        K_PIECE[K_SLOT[_s]] = len(V_PIECE) + len(K_PIECE)
K_SEQ = [(c, j) for c in range(4) for j in range(2)]
PIECES = sorted([(i, "v", s) for s, i in V_PIECE.items()] + [(i, "k", cj) for cj, i in K_PIECE.items()])
UNIT_PIECES = NT + 8
FIRST_PIECES = 8


def build(nc, xq, ctxT, mask, wqT, wkT, wvT, woT, bq, bk, bv, bo,
          aqT, akT, avT, aoT, gw, f1, f2, f3, fb, cosT, sinT, out):
    attn_dram = nc.dram_tensor("attn_scratch", (KC, P, B, LQ), F32).ap()
    base, loop, pro = ExitStack(), ExitStack(), ExitStack()

    def sb(ctx, name, shape, dt=F32):
        return ctx.enter_context(nc.sbuf_tensor(name, shape, dt))

    def sem(name):
        return base.enter_context(nc.semaphore(name))

    ident = sb(base, "ident", [P, P])
    gate = sb(base, "gate", [P, M])
    half_neg = sb(base, "half_neg", [P, M])
    bank = [base.enter_context(nc.psum_tensor(f"bank{i}", [P, 512], F32)) for i in range(8)]

    wk_h = sb(loop, "wk_h", [P, KC, D], F32R)
    wk_l = sb(loop, "wk_l", [P, KC, D], F32R)
    wv_h = sb(loop, "wv_h", [P, KC, D], F32R)
    wv_l = sb(loop, "wv_l", [P, KC, D], F32R)
    x_h = sb(loop, "x_h", [P, KC, S2P], F32R)
    x_l = sb(loop, "x_l", [P, KC, S2P], F32R)
    x_raw = sb(loop, "x_raw", [P, KC, 450])
    mask_u8 = sb(loop, "mask_u8", [P, S2P], U8)
    mask_f = sb(loop, "mask_f", [P, S2P], BF16)
    mask_b = sb(loop, "mask_b", [P, S2P], F16)
    bq_s = sb(loop, "bq_s", [P, KC])
    bk_s = sb(loop, "bk_s", [P, KC])
    bv_s = sb(loop, "bv_s", [64, KC, 2])
    qT = sb(loop, "qT", [P, 2, KC, T], F32R)
    q_bd = sb(loop, "q_bd", [P, PAIRS, 2, P], F32R)
    ks = sb(loop, "ks", [P, PAIRS, S2P], F32R)
    kf = sb(loop, "kf", [P, 2, 450])
    pt = sb(loop, "pt", [P, PTRING, PAIRS, 2, P], F32R)
    o_sb = sb(loop, "o_sb", [P, 2, 2, 2, P])
    o_fin = sb(loop, "o_fin", [64, 2, 2, P])
    o_out = sb(loop, "o_out", [P, 2, 2, LQ])
    smax = sb(loop, "smax", [P, PAIRS, 4])
    nmax = sb(loop, "nmax", [P, PAIRS])
    rsum = sb(loop, "rsum", [P, PAIRS])
    rinv = sb(loop, "rinv", [P, PAIRS])

    xs0 = sb(pro, "xs0", [P, M, D])
    xT0 = sb(pro, "xT0", [P, KC, T])
    w_raw = sb(pro, "w_raw", [P, KC, D])
    st0 = sb(pro, "st0", [P, M, 6])
    mv0 = sb(pro, "mv0", [P, M, 2])
    ve0 = sb(pro, "ve0", [P, M])
    rs0 = sb(pro, "rs0", [P, M])
    gate_u8 = sb(pro, "gate_u8", [P, M, S2], U8)
    q_tmp = sb(pro, "q_tmp", [P, T])
    pro.close()
    prob = sb(loop, "prob", [P, PAIRS, S2])
    v = sb(loop, "v", [P, VRING, PAIRS, 2, 64], F32R)
    loop.close()

    tail = ExitStack()
    bo_s = sb(tail, "bo_s", [P, D])
    fb_s = sb(tail, "fb_s", [P, D])
    cos_s = sb(tail, "cos_s", [P, D])
    sin_s = sb(tail, "sin_s", [P, D])
    gw_s = sb(tail, "gw_s", [P, 1])
    w = [sb(tail, f"w{i}", [P, KC, D]) for i in range(8)]
    aT = sb(tail, "aT", [P, KC, T])
    x1 = sb(tail, "x1", [P, M, D])
    xn = sb(tail, "xn", [P, M, D])
    xT = sb(tail, "xT", [P, KC, T])
    st1 = sb(tail, "st1", [P, M, 6])
    mv1 = sb(tail, "mv1", [P, M, 2])
    ve1 = sb(tail, "ve1", [P, M])
    rs1 = sb(tail, "rs1", [P, M])
    y_s = sb(tail, "y_s", [P, 2, D])
    qk = sb(tail, "qk", [P, 2, D])
    v_t = sb(tail, "v_t", [P, M, D])
    rot = sb(tail, "rot", [P, 2, D])
    feat = sb(tail, "feat", [P, 2, H, 2, HD])
    featT = sb(tail, "featT", [P, 2, 8, P])
    sc = sb(tail, "sc", [P, H, LQ])
    mx = sb(tail, "mx", [P, H])
    sm = sb(tail, "sm", [P, H])
    ri = sb(tail, "ri", [P, H])
    pb = sb(tail, "pb", [P, H, P])
    pbT = sb(tail, "pbT", [P, H, P])
    o_t = sb(tail, "o_t", [P, KC, P])
    o_q = sb(tail, "o_q", [P, KC, P])
    tail.close()

    ident_ok = sem("ident_ok")
    small_in, xq_in, wq_in, wk_in, wv_in = sem("small_in"), sem("xq_in"), sem("wq_in"), sem("wk_in"), sem("wv_in")
    raw_in = [sem(f"raw_in{k}") for k in range(KC)]
    mask_in = sem("mask_in")
    ln_stat, ln_pow, ln_done = sem("ln_stat"), sem("ln_pow"), sem("ln_done")
    pro_mm, pro_ev, q_step, q_done = sem("pro_mm"), sem("pro_ev"), sem("q_step"), sem("q_done")
    w_hi, w_lo = sem("w_hi"), sem("w_lo")
    gate_in, gate_ok = sem("gate_in"), sem("gate_ok")
    x_hi, x_lo = sem("x_hi"), sem("x_lo")
    mask_ok, bias_ok = sem("mask_ok"), sem("bias_ok")
    qbd_zero, qbd_ok = sem("qbd_zero"), sem("qbd_ok")
    pj_done, v_lo = sem("pj_done"), sem("v_lo")
    kf_ok, k_hi, k_lo = sem("kf_ok"), sem("k_hi"), sem("k_lo")
    sc_done, sc_free, nmax_ok = sem("sc_done"), sem("sc_free"), sem("nmax_ok")
    exp_ok, rinv_ok, norm_a, norm_v = sem("exp_ok"), sem("rinv_ok"), sem("norm_a"), sem("norm_v")
    v_hi = sem("v_hi")
    t_done, t_hi, t_lo = sem("t_done"), sem("t_hi"), sem("t_lo")
    pv_done = sem("pv_done")
    o_copy, o_add, o_shift, o_comb, o_ready = (sem("o_copy"), sem("o_add"), sem("o_shift"), sem("o_comb"),
                                               sem("o_ready"))
    o_stored = [sem("o_stored0"), sem("o_stored1")]
    t_in = sem("t_in")
    tw_in = [sem(f"tw_in{i}") for i in range(8)]
    at_in = sem("at_in")
    mm, ev = sem("mm"), sem("ev")
    t_stat, t_pow, t_norm = sem("t_stat"), sem("t_pow"), sem("t_norm")
    rope, feat_ok = sem("rope"), sem("feat_ok")
    caus, s_sub, s_exp, s_sum, pb_zero, pb_ok = (sem("caus"), sem("s_sub"), sem("s_exp"), sem("s_sum"),
                                                 sem("pb_zero"), sem("pb_ok"))
    y_bias, o_sq, a2_ok = sem("y_bias"), sem("o_sq"), sem("a2_ok")
    res1, res2, pre_tanh, tanh_ok, res3 = (sem("res1"), sem("res2"), sem("pre_tanh"), sem("tanh_ok"), sem("res3"))
    out_done = sem("out_done")

    def wait(eng, s, n):
        if isinstance(n, int) and n <= 0:
            return
        eng.wait_ge(s, n)

    def wait_apart(eng, *counts):
        counts = [(sm_, n if isinstance(n, int) else eng.to_reg(n)) for sm_, n in counts]
        eng.wait_ge(ident_ok, 2)
        for sm_, n in counts:
            wait(eng, sm_, n)

    def piece_base(u):
        return u * UNIT_PIECES + FIRST_PIECES

    def batches(eng, unit):
        unit(0, 0, False)
        unit(0, 1, False)
        with eng.Fori(1, B - 1) as b:
            unit(b, 0, False)
            unit(b, 1, False)
        unit(B - 1, 0, False)
        unit(B - 1, 1, True)

    J_Y1, J_T1, J_ATT = 0, M, 2 * M
    J_Y2 = J_ATT + 16 * M
    J_T2 = J_Y2 + M
    J_F1 = J_T2 + M
    J_F2, J_F3 = J_F1 + KC, J_F1 + 2 * KC

    def job(kind, m, i=0):
        return J_ATT + 16 * m + {"qkv": 0, "feat": 3, "score": 7, "prob": 11, "o": 15}[kind] + i

    block = base.enter_context(nc.Block())

    @block.sync
    def _(sp):
        sp.dma_start(xs0[:], xq.rearrange("(m p) d -> p m d", p=P)).then_inc(xq_in, 16)
        for dst, src in ((bq_s, bq), (bk_s, bk), (bv_s, bv)):
            sp.dma_start(dst[:], src).then_inc(small_in, 16)
        sp.dma_start(w_raw[:], wqT.rearrange("(k p) n -> p k n", p=P)).then_inc(wq_in, 16)

        def load_chunk(b, c):
            c0, n = CH[c]
            for k in range(KC):
                wait_apart(sp, (x_lo, (b * 4 + c - 1) * KC + k + 1))
                sp.dma_start(x_raw[:, k, 0:n], ctxT[b, k * P:(k + 1) * P, c0:c0 + n]).then_inc(raw_in[k], 16)

        def load_mask(b):
            wait_apart(sp, (bias_ok, b))
            sp.dma_start(mask_u8[:], mask[b].partition_broadcast(P)).then_inc(mask_in, 16)

        load_chunk(0, 0)
        load_mask(0)
        for b in range(B):
            sp.dma_start(gate_u8[64 * (b % 2):64 * (b % 2) + 64, b // 2, :], mask[b, 0:S2].partition_broadcast(64))\
                .then_inc(gate_in, 16)
        sp.wait_ge(pro_mm, M + KC)
        sp.dma_start(w_raw[:], wkT.rearrange("(k p) n -> p k n", p=P)).then_inc(wk_in, 16)
        sp.wait_ge(w_lo, 1)
        sp.dma_start(w_raw[:], wvT.rearrange("(k p) n -> p k n", p=P)).then_inc(wv_in, 16)
        for c in range(1, 4):
            load_chunk(0, c)

        def store(b, h):
            sp.dma_start(attn_dram[2 * h:2 * h + 2, :, b, :].rearrange("g p q -> p g q"), o_out[:, h, :, :])\
                .then_inc(o_stored[h], 16)

        def unit(b, h, last):
            u = b * 2 + h
            if h == 1 and not last:
                load_mask(b + 1)
                load_chunk(b + 1, 0)
                load_chunk(b + 1, 1)
            if h == 1:
                wait_apart(sp, (o_ready, u))
                store(b, 0)
            elif not (isinstance(b, int) and b == 0):
                wait_apart(sp, (o_ready, u))
                store(b - 1, 1)
            if h == 1 and not last:
                load_chunk(b + 1, 2)
                load_chunk(b + 1, 3)

        batches(sp, unit)
        sp.wait_ge(o_ready, 2 * B)
        store(B - 1, 1)
        sp.wait_ge(o_stored[0], 16 * B)
        sp.wait_ge(o_stored[1], 16 * B)
        sp.dma_start(aT[:], attn_dram.rearrange("k p b q -> p k (b q)")).then_inc(at_in, 16)
        order = (woT, aqT, akT, avT, aoT, f1, f2, f3)
        sp.dma_start(w[0][:], order[0].rearrange("(k p) n -> p k n", p=P)).then_inc(tw_in[0], 16)
        sp.dma_start(x1[:], xq.rearrange("(m p) d -> p m d", p=P)).then_inc(t_in, 16)
        sp.dma_start(bo_s[:], bo.partition_broadcast(P)).then_inc(t_in, 16)
        sp.dma_start(fb_s[:], fb.partition_broadcast(P)).then_inc(t_in, 16)
        sp.dma_start(cos_s[:], cosT).then_inc(t_in, 16)
        sp.dma_start(sin_s[:], sinT).then_inc(t_in, 16)
        sp.dma_start(gw_s[:], gw).then_inc(t_in, 16)
        for i in range(1, 8):
            sp.dma_start(w[i][:], order[i].rearrange("(k p) n -> p k n", p=P)).then_inc(tw_in[i], 16)
        for m in range(M):
            sp.wait_ge(res3, m + 1)
            sp.dma_start(out[m * P:(m + 1) * P, :], x1[:, m, :]).then_inc(out_done, 16)
        sp.wait_ge(out_done, 16 * M)

    @block.gpsimd
    def _(pool):
        pool.memset(ident[:], 0.0).then_inc(ident_ok, 1)
        pool.wait_ge(ident_ok, 1)
        pool.affine_select(out=ident[:], in_=ident[:], compare_op=ALU.not_equal, fill=1.0, base=0,
                           pattern=[[-1, P]], channel_multiplier=1).then_inc(ident_ok, 1)
        pool.memset(half_neg[:], -0.5).then_inc(ln_pow, 1)
        pool.memset(q_bd[:].bitcast(F32), 0.0).then_inc(qbd_zero, 1)
        pool.wait_ge(ln_pow, 1)
        for m in range(M):
            pool.wait_ge(ln_stat, 3 * m + 3)
            pool.tensor_tensor(rs0[:, m:m + 1], ve0[:, m:m + 1], half_neg[:, m:m + 1], ALU.pow).then_inc(ln_pow, 1)

        def split_chunk(b, c):
            c0, n = CH[c]
            for k in range(KC):
                pool.wait_ge(x_hi, (b * 4 + c) * KC + k + 1)
                pool.tensor_tensor(x_l[:, k, c0:c0 + n], x_raw[:, k, 0:n], x_h[:, k, c0:c0 + n].bitcast(F32),
                                   ALU.subtract).then_inc(x_lo, 1)

        def make_mask(b):
            wait_apart(pool, (mask_in, b * 16 + 16), (kf_ok, b * 16))
            pool.tensor_copy(mask_f[:], mask_u8[:]).then_inc(mask_ok, 1)

        def make_bias(b):
            wait_apart(pool, (sc_free, b * 32), (mask_ok, b + 1))
            pool.tensor_scalar(mask_b[:], mask_f[:], -FILL, FILL, ALU.mult, ALU.add).then_inc(bias_ok, 1)

        split_chunk(0, 0)
        make_mask(0)
        make_bias(0)
        for c in range(1, 4):
            split_chunk(0, c)

        def unit(b, h, last):
            if h == 1 and not last:
                make_mask(b + 1)
                make_bias(b + 1)
                for c in range(4):
                    split_chunk(b + 1, c)

        batches(pool, unit)

        def inv_std(n):
            for m in range(M):
                pool.wait_ge(t_stat, n * 3 * M + 3 * m + 3)
                pool.tensor_tensor(rs1[:, m:m + 1], ve1[:, m:m + 1], half_neg[:, m:m + 1], ALU.pow).then_inc(t_pow, 1)

        pool.wait_ge(at_in, 16)
        pool.memset(pb[:], 0.0).then_inc(pb_zero, 1)
        inv_std(0)
        for m in range(M):
            pool.wait_ge(ev, job("score", m, 3) + 1)
            for r in range(2):
                pool.affine_select(out=sc[64 * r:64 * r + 64], in_=sc[64 * r:64 * r + 64], compare_op=ALU.is_ge,
                                   fill=-1e9, base=0, pattern=[[0, H], [-1, LQ]], channel_multiplier=1)\
                    .then_inc(caus, 1)
        inv_std(1)

    @block.scalar
    def _(act):
        for m in range(M):
            act.wait_ge(pro_mm, m + 1)
            act.activation(xT0[:, :, m * P:(m + 1) * P], bank[4 + m][:].rearrange("p (k t) -> p k t", k=KC), ACT.Copy)\
                .then_inc(pro_ev, 1)

        def split_chunk(b, c):
            c0, n = CH[c]
            for k in range(KC):
                act.wait_ge(raw_in[k], (b * 4 + c) * 16 + 16)
                if not (isinstance(b, int) and b == 0):
                    act.wait_ge(pj_done, piece_base(b * 2 - 1) + V_PIECE[CHUNK_END[c] - 1] + 1)
                act.activation(x_h[:, k, c0:c0 + n], x_raw[:, k, 0:n], ACT.Copy).then_inc(x_hi, 1)

        split_chunk(0, 0)
        act.wait_ge(wk_in, 16)
        act.activation(wk_h[:], w_raw[:], ACT.Copy).then_inc(w_hi, 1)
        act.wait_ge(wv_in, 16)
        act.activation(wv_h[:], w_raw[:], ACT.Copy).then_inc(w_hi, 1)
        for c in range(1, 4):
            split_chunk(0, c)

        def q_blocks(b, h, u):
            wait(act, sc_done, u * 16)
            for r in range(4):
                for par in range(2):
                    src = 32 * (r % 2) + 64 * par
                    a = act.activation(
                        q_bd[32 * r:32 * r + 32, par::2, :, 64 * (r % 2):64 * (r % 2) + 64],
                        qT[src:src + 32, :, 2 * h:2 * h + 2, bass.ds(b * LQ, LQ)].bitcast(F32)
                        .rearrange("p l g q -> p g l q"), ACT.Copy)
            a.then_inc(qbd_ok, 1)

        def key_hi(n):
            c, j, count = n
            c0, w_ = CH[c]
            act.wait_ge(kf_ok, count + 1)
            sl = K_SEQ.index((c, j)) % 2
            act.activation(ks[0:64, 2 * j, c0:c0 + w_], kf[0:64, sl, 0:w_], ACT.Copy).then_inc(k_hi, 1)
            act.activation(ks[64:128, 2 * j + 1, c0:c0 + w_], kf[64:128, sl, 0:w_], ACT.Copy).then_inc(k_hi, 1)

        act.wait_ge(qbd_zero, 1)
        act.wait_ge(q_done, KC)
        q_blocks(0, 0, 0)
        for i, (c, j) in enumerate(K_SEQ):
            key_hi((c, j, i))

        def exp_pair(u, p):
            act.wait_ge(nmax_ok, u * PAIRS + p + 1)
            act.activation(prob[:, p, :], prob[:, p, :], ACT.Exp, bias=nmax[:, p:p + 1], scale=1.0,
                           accum_out=rsum[:, p:p + 1]).then_inc(exp_ok, 1)

        def norm_pair(u, p):
            act.wait_ge(rinv_ok, u * PAIRS + p + 1)
            act.activation(prob[:, p, :], prob[:, p, :], ACT.Copy, scale=rinv[:, p:p + 1]).then_inc(norm_a, 1)

        def out_copy(u):
            act.wait_ge(pv_done, (u + 1) * NT)
            wait(act, o_comb, u)
            for j in range(2):
                act.activation(o_sb[:, j].rearrange("p a l q -> p (a l q)"), bank[6 + j][:], ACT.Copy).then_inc(o_copy, 1)

        def out_shift(u):
            act.wait_ge(o_add, (u + 1) * 2)
            wait(act, o_ready, u)
            act.activation(o_fin[:], o_sb[64:128, :, :, 0, :], ACT.Copy).then_inc(o_shift, 1)

        def unit(b, h, last):
            u = b * 2 + h
            first = isinstance(b, int) and b == 0 and h == 0
            for s in range(SLOTS):
                if s < NT:
                    act.wait_ge(pj_done, piece_base(u) + (s if last else V_PIECE[s]) + 1)
                    prev = u * NT + s - VRING + 1 if s >= VRING else (u - 1) * NT + \
                        (s + VRING if s + VRING < NT else s) + 1
                    wait(act, pv_done, prev)
                    r = ROWS[s]
                    pj = bank[((s if last else V_PIECE[s]) + h) % 2]
                    act.activation(v[0:r, s % VRING, :, 0, :], pj[0:r, 0:256].rearrange("p (a d) -> p a d", a=PAIRS),
                                   ACT.Copy).then_inc(v_hi, 1)
                if s < 4:
                    exp_pair(u, s)
                if s in (2, 3):
                    norm_pair(u, s - 2)
                if 0 <= s - T_LAG < NT:
                    t = s - T_LAG
                    r = ROWS[t]
                    act.wait_ge(t_done, u * NT + t + 1)
                    wait(act, pv_done, u * NT + t - PTRING + 1 if t >= PTRING else (u - 1) * NT +
                         max(i for i in range(NT) if i % PTRING == t) + 1)
                    act.activation(pt[0:r, t % PTRING, :, 0, :], bank[4 + t % 2][0:r, :].rearrange("p (a q) -> p a q", a=PAIRS),
                                   ACT.Copy).then_inc(t_hi, 1)
                if s in K_SLOT and not last:
                    c, j = K_SLOT[s]
                    if (c, j) == (0, 0):
                        act.wait_ge(sc_done, (u + 1) * 16)
                    key_hi((c, j, (u + 1) * 8 + K_SEQ.index((c, j))))
                if s == 4 and not first:
                    out_copy(u - 1)
                if s == 5 and not first:
                    out_shift(u - 1)
                if s == 7 and not last:
                    if h == 0:
                        q_blocks(b, 1, u + 1)
                    else:
                        q_blocks(b + 1, 0, u + 1)
                if s in XH_SLOT and h == 1 and not last:
                    split_chunk(b + 1, XH_SLOT[s])

        batches(act, unit)
        out_copy(2 * B - 1)
        out_shift(2 * B - 1)

        act.wait_ge(at_in, 16)
        n_ev = [0]

        def take(dst, src):
            act.wait_ge(mm, n_ev[0] + 1)
            i = act.activation(dst, src, ACT.Copy)
            i.then_inc(ev, 1)
            n_ev[0] += 1

        def bk_of(n):
            return bank[n % 8]

        for m in range(M):
            if m >= 2:
                act.wait_ge(res1, m - 1)
            take(y_s[:, m % 2, :], bk_of(J_Y1 + m)[:])
        for m in range(M):
            take(xT[:, :, m * P:(m + 1) * P], bk_of(J_T1 + m)[:].rearrange("p (k t) -> p k t", k=KC))
        for m in range(M):
            for i in range(3):
                if i < 2 and m > 0:
                    act.wait_ge(rope, 6 * m)
                take(qk[:, i, :] if i < 2 else v_t[:, m, :], bk_of(job("qkv", m, i))[:])
            for f in range(2):
                for q4 in range(2):
                    take(featT[:, f, 4 * q4:4 * q4 + 4, :], bk_of(job("feat", m, 2 * f + q4))[:].rearrange("p (a t) -> p a t", a=4))
            if m > 0:
                act.wait_ge(pb_ok, 2 * m)
            for i in range(4):
                src = bk_of(job("score", m, i))[:].rearrange("p (a t) -> p a t", a=4)
                h0 = 8 * (i % 2) + i // 2
                act.wait_ge(mm, job("score", m, i) + 1)
                act.activation(sc[0:64, h0:h0 + 7:2, :], src[0:64, :, 0:64], ACT.Copy)
                act.activation(sc[64:128, h0:h0 + 7:2, :], src[64:128, :, 64:128], ACT.Copy).then_inc(ev, 1)
                n_ev[0] += 1
            act.wait_ge(s_sub, 2 * m + 2)
            act.activation(sc[:], sc[:], ACT.Exp).then_inc(s_exp, 1)
            for i in range(4):
                take(pbT[:, 4 * i:4 * i + 4, :], bk_of(job("prob", m, i))[:].rearrange("p (a t) -> p a t", a=4))
            if m > 0:
                act.wait_ge(a2_ok, m)
            take(o_t[:], bk_of(job("o", m))[:].rearrange("p (k t) -> p k t", k=KC))
        for m in range(M):
            if m >= 2:
                act.wait_ge(res2, m - 1)
            take(y_s[:, m % 2, :], bk_of(J_Y2 + m)[:])
        for m in range(M):
            take(xT[:, :, m * P:(m + 1) * P], bk_of(J_T2 + m)[:].rearrange("p (k t) -> p k t", k=KC))
        for g in range(KC):
            take(aT[:, g, :], bk_of(J_F1 + g)[:])
        act.wait_ge(mm, J_F2 + KC)
        for g in range(KC):
            take(xT[:, g, :], bk_of(J_F2 + g)[:])
        for m in range(M):
            take(xn[:, m, :], bk_of(J_F3 + m)[:])
        for m in range(M):
            act.wait_ge(pre_tanh, m + 1)
            act.activation(xn[:, m, :], xn[:, m, :], ACT.Tanh).then_inc(tanh_ok, 1)

    @block.vector
    def _(dve):
        for m in range(M):
            if m == 0:
                dve.wait_ge(xq_in, 16)
            dve.bn_stats(st0[:, m, :], xs0[:, m, :]).then_inc(ln_stat, 1)
            dve.wait_ge(ln_stat, 3 * m + 1)
            dve.bn_aggr(mv0[:, m, :], st0[:, m, :]).then_inc(ln_stat, 1)
            dve.wait_ge(ln_stat, 3 * m + 2)
            dve.tensor_scalar(ve0[:, m:m + 1], mv0[:, m, 1:2], EPS, None, ALU.add).then_inc(ln_stat, 1)
        for m in range(M):
            dve.wait_ge(ln_pow, m + 2)
            dve.tensor_scalar(xs0[:, m, :], xs0[:, m, :], mv0[:, m, 0:1], rs0[:, m:m + 1],
                              ALU.subtract, ALU.mult).then_inc(ln_done, 1)
        dve.wait_ge(small_in, 48)
        for g in range(KC):
            dve.wait_ge(pro_mm, M + g + 1)
            dve.tensor_scalar(q_tmp[:], bank[g][:], bq_s[:, g:g + 1], XSCALE, ALU.add, ALU.mult).then_inc(q_step, 1)
            dve.wait_ge(q_step, 2 * g + 1)
            dve.tensor_copy(qT[:, 0, g, :], q_tmp[:]).then_inc(q_step, 1)
            dve.wait_ge(q_step, 2 * g + 2)
            dve.tensor_tensor(qT[:, 1, g, :], q_tmp[:], qT[:, 0, g, :].bitcast(F32), ALU.subtract).then_inc(q_done, 1)
            dve.wait_ge(q_done, g + 1)
        dve.wait_ge(gate_in, 16 * B)
        dve.tensor_reduce(gate[:], gate_u8[:], AX.X, ALU.max).then_inc(gate_ok, 1)
        dve.wait_ge(w_hi, 1)
        dve.tensor_tensor(wk_l[:], w_raw[:], wk_h[:].bitcast(F32), ALU.subtract).then_inc(w_lo, 1)
        dve.wait_ge(w_hi, 2)
        dve.tensor_tensor(wv_l[:], w_raw[:], wv_h[:].bitcast(F32), ALU.subtract).then_inc(w_lo, 1)

        def key_full(c, j, count, piece, g, par, b):
            c0, n = CH[c]
            dve.wait_ge(pj_done, piece + 1)
            sl = K_SEQ.index((c, j)) % 2
            if K_SEQ.index((c, j)) == 0:
                dve.wait_ge(mask_ok, b + 1)
            wait(dve, k_lo, 2 * (count - 1))
            dve.scalar_tensor_tensor(kf[:, sl, 0:n], bank[par][:, 0:n], bk_s[:, g:g + 1], mask_f[:, c0:c0 + n],
                                     ALU.add, ALU.mult).then_inc(kf_ok, 1)

        def key_lo(c, j, count):
            c0, n = CH[c]
            sl = K_SEQ.index((c, j)) % 2
            dve.wait_ge(k_hi, 2 * count + 2)
            dve.tensor_tensor(ks[64:128, 2 * j, c0:c0 + n], kf[0:64, sl, 0:n], ks[0:64, 2 * j, c0:c0 + n].bitcast(F32),
                              ALU.subtract).then_inc(k_lo, 1)
            dve.tensor_tensor(ks[0:64, 2 * j + 1, c0:c0 + n], kf[64:128, sl, 0:n],
                              ks[64:128, 2 * j + 1, c0:c0 + n].bitcast(F32), ALU.subtract).then_inc(k_lo, 1)

        for i, (c, j) in enumerate(K_SEQ):
            key_full(c, j, i, i, j, i % 2, 0)
            key_lo(c, j, i)

        def score_pair(u, p):
            if p == 0:
                wait(dve, t_done, u * NT)
            for c in range(4):
                c0, n = CH[c]
                n = min(n, S2 - c0)
                wait_apart(dve, (sc_done, u * 16 + 4 * p + c + 1))
                dve.tensor_tensor_reduce(prob[:, p, c0:c0 + n], bank[2 + c % 2][:, 0:n], mask_b[:, c0:c0 + n], 1.0, -3.0e38,
                                         ALU.add, ALU.max, smax[:, p, c:c + 1]).then_inc(sc_free, 1)
            dve.wait_ge(sc_free, u * 16 + 4 * p + 4)
            dve.tensor_reduce(nmax[:, p:p + 1], smax[:, p, :], AX.X, ALU.max, negate=True).then_inc(nmax_ok, 1)

        def recip(u, p):
            dve.wait_ge(exp_ok, u * PAIRS + p + 1)
            dve.reciprocal(rinv[:, p:p + 1], rsum[:, p:p + 1]).then_inc(rinv_ok, 1)

        def norm_pair(u, p):
            dve.wait_ge(rinv_ok, u * PAIRS + p + 1)
            dve.tensor_scalar(prob[:, p, :], prob[:, p, :], rinv[:, p:p + 1], None, ALU.mult).then_inc(norm_v, 1)

        def out_add(u):
            for j in range(2):
                dve.wait_ge(o_copy, u * 2 + j + 1)
                dve.tensor_tensor(o_sb[:, j, :, 0, :], o_sb[:, j, :, 0, :], o_sb[:, j, :, 1, :], ALU.add).then_inc(o_add, 1)

        def out_combine(u, b, h):
            dve.wait_ge(o_shift, u + 1)
            dve.tensor_tensor(o_fin[:], o_sb[0:64, :, :, 0, :], o_fin[:], ALU.add).then_inc(o_comb, 1)
            dve.wait_ge(o_comb, u + 1)
            wait(dve, o_stored[h], b * 16)
            for a in range(2):
                for i in range(2):
                    for j in range(2):
                        r = 64 * a + 32 * i
                        g = 2 * h + j
                        op = dve.tensor_scalar(o_out[r:r + 32, h, j, :], o_fin[32 * i:32 * i + 32, j, a, 64 * i:64 * i + 64],
                                               bv_s[32 * i:32 * i + 32, g, a:a + 1], None, ALU.add)
            op.then_inc(o_ready, 1)

        def unit(b, h, last):
            u = b * 2 + h
            first = isinstance(b, int) and b == 0 and h == 0
            for s in range(SLOTS):
                if s < 4:
                    if s == 0 and h == 0:
                        dve.wait_ge(bias_ok, b + 1)
                    score_pair(u, s)
                if s < NT:
                    dve.wait_ge(v_hi, u * NT + s + 1)
                    r = ROWS[s]
                    pj = bank[((s if last else V_PIECE[s]) + h) % 2]
                    dve.tensor_tensor(v[0:r, s % VRING, :, 1, :], pj[0:r, 0:256].rearrange("p (a d) -> p a d", a=PAIRS),
                                      v[0:r, s % VRING, :, 0, :].bitcast(F32), ALU.subtract).then_inc(v_lo, 1)
                if 1 <= s <= 4:
                    recip(u, s - 1)
                if s in (3, 4):
                    norm_pair(u, s - 1)
                if s in K_SLOT and not last:
                    c, j = K_SLOT[s]
                    nb, nh = (b, 1) if h == 0 else (b + 1, 0)
                    i = K_SEQ.index((c, j))
                    key_full(c, j, (u + 1) * 8 + i, piece_base(u) + K_PIECE[(c, j)], 2 * nh + j,
                             (K_PIECE[(c, j)] + h) % 2, nb)
                if 0 <= s - T_LAG < NT:
                    t = s - T_LAG
                    r = ROWS[t]
                    dve.wait_ge(t_hi, u * NT + t + 1)
                    dve.tensor_tensor(pt[0:r, t % PTRING, :, 1, :], bank[4 + t % 2][0:r, :].rearrange("p (a q) -> p a q", a=PAIRS),
                                      pt[0:r, t % PTRING, :, 0, :].bitcast(F32), ALU.subtract).then_inc(t_lo, 1)
                if s in K_SLOT and not last:
                    key_lo(c, j, (u + 1) * 8 + i)
                if s == 4 and not first:
                    out_add(u - 1)
                if s == 6 and not first:
                    out_combine(u - 1, b - 1 if h == 0 else b, 1 - h)

        batches(dve, unit)
        out_add(2 * B - 1)
        out_combine(2 * B - 1, B - 1, 1)

        dve.wait_ge(t_in, 16 * 6)

        def layer_norm(n):
            for m in range(M):
                c = n * 3 * M + 3 * m
                dve.bn_stats(st1[:, m, :], x1[:, m, :]).then_inc(t_stat, 1)
                dve.wait_ge(t_stat, c + 1)
                dve.bn_aggr(mv1[:, m, :], st1[:, m, :]).then_inc(t_stat, 1)
                dve.wait_ge(t_stat, c + 2)
                dve.tensor_scalar(ve1[:, m:m + 1], mv1[:, m, 1:2], EPS, None, ALU.add).then_inc(t_stat, 1)
            for m in range(M):
                dve.wait_ge(t_pow, n * M + m + 1)
                dve.tensor_scalar(xn[:, m, :], x1[:, m, :], mv1[:, m, 0:1], rs1[:, m:m + 1],
                                  ALU.subtract, ALU.mult).then_inc(t_norm, 1)

        dve.wait_ge(gate_ok, 1)
        for m in range(M):
            dve.wait_ge(ev, J_Y1 + m + 1)
            dve.tensor_tensor(y_s[:, m % 2, :], y_s[:, m % 2, :], bo_s[:], ALU.add).then_inc(y_bias, 1)
            dve.wait_ge(y_bias, m + 1)
            dve.scalar_tensor_tensor(x1[:, m, :], y_s[:, m % 2, :], gate[:, m:m + 1], x1[:, m, :],
                                     ALU.mult, ALU.add).then_inc(res1, 1)
            dve.wait_ge(res1, m + 1)
        layer_norm(0)
        q_scale = HD ** -0.5
        for m in range(M):
            for i in range(2):
                n = 6 * m + 3 * i
                dve.wait_ge(ev, job("qkv", m, i) + 1)
                src = qk[:, i, :].rearrange("p (h d) -> p h d", h=H)
                dst = rot[:, i, :].rearrange("p (h d) -> p h d", h=H)
                sn = sin_s[:].rearrange("p (h d) -> p h d", h=H)
                if m > 0 and i == 0:
                    dve.wait_ge(feat_ok, 4 * m)
                dve.tensor_tensor(dst[:, :, 0:16], src[:, :, 16:32], sn[:, :, 0:16], ALU.mult)
                dve.tensor_tensor(dst[:, :, 16:32], src[:, :, 0:16], sn[:, :, 16:32], ALU.mult).then_inc(rope, 1)
                dve.wait_ge(rope, n + 1)
                dve.tensor_tensor(qk[:, i, :], qk[:, i, :], cos_s[:], ALU.mult).then_inc(rope, 1)
                dve.wait_ge(rope, n + 2)
                dve.tensor_tensor(rot[:, i, :], rot[:, i, :], qk[:, i, :], ALU.add).then_inc(rope, 1)
                dve.wait_ge(rope, n + 3)
                if m > 0:
                    dve.wait_ge(mm, job("feat", m - 1, 3) + 1)
                one, two = (q_scale, 0.1 * q_scale) if i == 0 else (1.0, 1.0)
                dve.tensor_scalar(feat[:, i, :, 0, :], dst, one, None, ALU.mult).then_inc(feat_ok, 1)
                dve.scalar_tensor_tensor(feat[:, i, :, 1, :], dst, two, dst, ALU.mult, ALU.mult).then_inc(feat_ok, 1)
            dve.wait_ge(caus, 2 * m + 2)
            dve.tensor_reduce(mx[:], sc[:], AX.X, ALU.max).then_inc(s_sub, 1)
            dve.wait_ge(s_sub, 2 * m + 1)
            dve.tensor_tensor(sc[:], sc[:], mx[:].unsqueeze(2).to_broadcast([P, H, LQ]), ALU.subtract).then_inc(s_sub, 1)
            dve.wait_ge(s_exp, m + 1)
            dve.tensor_reduce(sm[:], sc[:], AX.X, ALU.add).then_inc(s_sum, 1)
            dve.wait_ge(s_sum, 2 * m + 1)
            dve.reciprocal(ri[:], sm[:]).then_inc(s_sum, 1)
            dve.wait_ge(s_sum, 2 * m + 2)
            if m == 0:
                dve.wait_ge(pb_zero, 1)
            else:
                dve.wait_ge(mm, job("prob", m - 1, 3) + 1)
            for r in range(2):
                rr = slice(64 * r, 64 * r + 64)
                dve.tensor_tensor(pb[rr, :, 64 * r:64 * r + 64], sc[rr], ri[rr].unsqueeze(2).to_broadcast([64, H, LQ]),
                                  ALU.mult).then_inc(pb_ok, 1)
            dve.wait_ge(ev, job("o", m) + 1)
            dve.scalar_tensor_tensor(o_q[:], o_t[:], gw_s[:, 0:1], o_t[:], ALU.mult, ALU.mult).then_inc(o_sq, 1)
            dve.wait_ge(o_sq, m + 1)
            dve.scalar_tensor_tensor(aT[:, :, m * P:(m + 1) * P], o_q[:], 0.05, o_t[:], ALU.mult, ALU.add)\
                .then_inc(a2_ok, 1)
        for m in range(M):
            dve.wait_ge(ev, J_Y2 + m + 1)
            dve.tensor_tensor(x1[:, m, :], x1[:, m, :], y_s[:, m % 2, :], ALU.add).then_inc(res2, 1)
            dve.wait_ge(res2, m + 1)
        layer_norm(1)
        for m in range(M):
            dve.wait_ge(ev, J_F3 + m + 1)
            dve.tensor_tensor(xn[:, m, :], xn[:, m, :], fb_s[:], ALU.add).then_inc(pre_tanh, 1)
        for m in range(M):
            dve.wait_ge(tanh_ok, m + 1)
            dve.tensor_tensor(x1[:, m, :], x1[:, m, :], xn[:, m, :], ALU.add).then_inc(res3, 1)

    @block.tensor
    def _(pe):
        pe.wait_ge(ident_ok, 2)
        for m in range(M):
            pe.wait_ge(ln_done, m + 1)
            for k in range(KC):
                t = pe.transpose(bank[4 + m][:, k * P:(k + 1) * P], xs0[:, m, k * P:(k + 1) * P], ident[:])
            t.then_inc(pro_mm, 1)
        pe.wait_ge(pro_ev, M)
        pe.wait_ge(wq_in, 16)
        for g in range(KC):
            for k in range(KC):
                q = pe.matmul(bank[g][:], w_raw[:, k, g * P:(g + 1) * P], xT0[:, k, :], start=(k == 0), stop=(k == KC - 1))
            q.then_inc(pro_mm, 1)
        pe.wait_ge(q_done, KC)
        pe.wait_ge(w_lo, 1)

        def key_piece(c, j, b, h, bk):
            c0, n = CH[c]
            g = slice((2 * h + j) * P, (2 * h + j + 1) * P)
            if h == 0 and j == 0:
                pe.wait_ge(x_lo, b * 16 + 4 * (c + 1))
            passes = [(w_, x, k) for k in range(KC) for w_, x in ((wk_h, x_h), (wk_h, x_l), (wk_l, x_h))]
            for i, (w_, x, k) in enumerate(passes):
                mm_ = pe.matmul(bank[bk][:, 0:n], w_[:, k, g], x[:, k, c0:c0 + n],
                                start=(i == 0), stop=(i == len(passes) - 1))
            mm_.then_inc(pj_done, 1)

        for i, (c, j) in enumerate(K_SEQ):
            wait(pe, kf_ok, i - 1)
            key_piece(c, j, 0, 0, i % 2)
        pe.wait_ge(w_lo, 2)

        def bank_free(u, i, last):
            if last and i >= 2:
                pe.wait_ge(v_lo, u * NT + i - 1)
            elif i < 2:
                pe.wait_ge(kf_ok, u * 8 + 7 + i)
            else:
                _, kind, what = PIECES[i - 2]
                if kind == "v":
                    pe.wait_ge(v_lo, u * NT + what + 1)
                else:
                    pe.wait_ge(kf_ok, (u + 1) * 8 + K_SEQ.index(what) + 1)

        def score_pair(u, p):
            if p == 0:
                pe.wait_ge(qbd_ok, u + 1)
            for c in range(4):
                c0, n = CH[c]
                pe.wait_ge(k_lo, u * 16 + 2 * (2 * c + p // 2 + 1))
                wait(pe, sc_free, u * 16 + 4 * p + c - 1)
                for l in range(2):
                    s_ = pe.matmul(bank[2 + c % 2][:, 0:n], q_bd[:, p, 1 - l, :], ks[:, p, c0:c0 + n],
                                   start=(l == 0), stop=(l == 1))
                s_.then_inc(sc_done, 1)

        def value_tile(u, h, s, last):
            i = s if last else V_PIECE[s]
            bank_free(u, i, last)
            r = ROWS[s]
            t0 = s * P
            passes = [(x, w_, k) for k in range(KC) for x, w_ in ((x_h, wv_h), (x_h, wv_l), (x_l, wv_h))]
            for n, (x, w_, k) in enumerate(passes):
                v_ = pe.matmul(bank[(i + h) % 2][0:r, 0:256], x[:, k, t0:t0 + r], w_[:, k, 256 * h:256 * h + 256],
                               start=(n == 0), stop=(n == len(passes) - 1))
            v_.then_inc(pj_done, 1)

        def turn_tile(u, t):
            r = ROWS[t]
            if t == 0:
                pe.wait_ge(norm_a, (u + 1) * 2)
                pe.wait_ge(norm_v, (u + 1) * 2)
            wait(pe, t_lo, u * NT + t - 1 if t >= 2 else u * NT - t)
            for p in range(PAIRS):
                t_ = pe.transpose(bank[4 + t % 2][0:r, p * P:(p + 1) * P], prob[:, p, t * P:t * P + r], ident[:])
            t_.then_inc(t_done, 1)

        def product_tile(u, t):
            r = ROWS[t]
            if t == 0:
                wait(pe, o_copy, u * 2)
            pe.wait_ge(v_lo, u * NT + t + 1)
            pe.wait_ge(t_lo, u * NT + t + 1)
            for p in range(PAIRS):
                o_ = pe.matmul(bank[6 + p // 2][:, 256 * (p % 2):256 * (p % 2) + 256], v[0:r, t % VRING, p, :, :],
                               pt[0:r, t % PTRING, p, :, :], start=(t == 0 and p % 2 == 0), stop=(t == NT - 1),
                               skip_group_check=True)
            o_.then_inc(pv_done, 1)

        def unit(b, h, last):
            u = b * 2 + h
            for s in range(SLOTS):
                if s < 4:
                    score_pair(u, s)
                if s < NT:
                    value_tile(u, h, s, last)
                if s in K_SLOT and not last:
                    c, j = K_SLOT[s]
                    i = K_PIECE[(c, j)]
                    bank_free(u, i, last)
                    key_piece(c, j, b if h == 0 else b + 1, 1 - h, (i + h) % 2)
                if 0 <= s - T_LAG < NT:
                    turn_tile(u, s - T_LAG)
                if 0 <= s - PV_LAG < NT:
                    product_tile(u, s - PV_LAG)

        batches(pe, unit)

        n_mm = [0]

        def begin():
            if n_mm[0] >= 8:
                pe.wait_ge(ev, n_mm[0] - 7)
            return bank[n_mm[0] % 8]

        def done(i):
            i.then_inc(mm, 1)
            n_mm[0] += 1

        def rows_product(xt, wt, m):
            bk = begin()
            for k in range(KC):
                i = pe.matmul(bk[:], xt[:, k, m * P:(m + 1) * P], wt[:, k, :], start=(k == 0), stop=(k == KC - 1))
            done(i)

        def cols_product(wt, xt, g):
            bk = begin()
            for k in range(KC):
                i = pe.matmul(bk[:], wt[:, k, g * P:(g + 1) * P], xt[:, k, :], start=(k == 0), stop=(k == KC - 1))
            done(i)

        def turn4(src):
            bk = begin()
            for i in range(4):
                t_ = pe.transpose(bk[:, i * P:(i + 1) * P], src(i), ident[:])
            done(t_)

        pe.wait_ge(o_copy, 4 * B)
        pe.wait_ge(at_in, 16)
        pe.wait_ge(tw_in[0], 16)
        for m in range(M):
            rows_product(aT, w[0], m)
        for m in range(M):
            pe.wait_ge(t_norm, m + 1)
            turn4(lambda i: xn[:, m, i * P:(i + 1) * P])
        for m in range(M):
            pe.wait_ge(ev, J_T1 + m + 1)
            for i in range(3):
                pe.wait_ge(tw_in[1 + i], 16)
                rows_product(xT, w[1 + i], m)
            for f in range(2):
                pe.wait_ge(feat_ok, 4 * m + 2 * f + 2)
                flat = feat[:, f].rearrange("p h s d -> p (h s d)")
                for q4 in range(2):
                    turn4(lambda i: flat[:, (4 * q4 + i) * P:(4 * q4 + i + 1) * P])
            pe.wait_ge(ev, job("feat", m, 3) + 1)
            for i in range(4):
                bk = begin()
                r = 64 * (i // 2)
                for a in range(4):
                    hp = 4 * (i % 2) + a
                    s_ = pe.matmul(bk[:, a * P:(a + 1) * P], featT[r:r + 64, 0, hp, :], featT[r:r + 64, 1, hp, :],
                                   start=True, stop=True)
                done(s_)
            pe.wait_ge(pb_ok, 2 * m + 2)
            for i in range(4):
                turn4(lambda a: pb[:, 4 * i + a, :])
            pe.wait_ge(ev, job("prob", m, 3) + 1)
            bk = begin()
            for hd in range(H):
                r = 32 * (hd % 4)
                o_ = pe.matmul(bk[r:r + 32, (hd // 4) * P:(hd // 4 + 1) * P], v_t[:, m, HD * hd:HD * hd + HD], pbT[:, hd, :],
                               start=True, stop=True)
            done(o_)
        pe.wait_ge(tw_in[4], 16)
        for m in range(M):
            pe.wait_ge(a2_ok, m + 1)
            rows_product(aT, w[4], m)
        for m in range(M):
            pe.wait_ge(t_norm, M + m + 1)
            turn4(lambda i: xn[:, m, i * P:(i + 1) * P])
        pe.wait_ge(ev, J_T2 + M)
        pe.wait_ge(tw_in[5], 16)
        for g in range(KC):
            cols_product(w[5], xT, g)
        pe.wait_ge(ev, J_F1 + KC)
        pe.wait_ge(tw_in[6], 16)
        for g in range(KC):
            cols_product(w[6], aT, g)
        pe.wait_ge(ev, J_F2 + KC)
        pe.wait_ge(tw_in[7], 16)
        for m in range(M):
            rows_product(xT, w[7], m)

    base.close()
    return nc


def kernel(x, ctx_1024, mask_BxS2_bk1, L0_xattn_Wq, L0_xattn_bq, L0_xattn_Wk, L0_xattn_bk, L0_xattn_Wv, L0_xattn_bv,
           L0_xattn_Wo, L0_xattn_bo, L0_attn_Wq, L0_attn_Wk, L0_attn_Wv, L0_attn_Wo, L0_attn_gate_w, L0_ffn_weight,
           L0_ffn_aux_weight1, L0_ffn_aux_weight2, L0_ffn_bias):
    import concourse.bacc as bacc
    from concourse.bass_utils import run_bass_kernel_spmd

    def tr(a):
        return np.ascontiguousarray(np.asarray(a).T)

    def cols(a):
        return np.ascontiguousarray(np.asarray(a).reshape(KC, P).T)

    ctx = np.asarray(ctx_1024)
    ctxT = np.zeros((B, D, S2P), ctx.dtype)
    ctxT[:, :, :S2] = ctx.transpose(0, 2, 1)
    mask = np.zeros((B, S2P), bool)
    mask[:, :S2] = np.asarray(mask_BxS2_bk1)

    half = HD // 2
    inv = (1.0 / np.float32(10000.0) ** (np.arange(half, dtype=np.float32) / np.float32(half))).astype(np.float32)
    ang = (np.arange(LQ, dtype=np.float32)[:, None] * inv[None, :]).astype(np.float32)
    cos, sin = np.cos(ang).astype(np.float32), np.sin(ang).astype(np.float32)
    cosT = np.ascontiguousarray(np.tile(np.concatenate([cos, cos], 1), (P // LQ, H)))
    sinT = np.ascontiguousarray(np.tile(np.concatenate([-sin, sin], 1), (P // LQ, H)))

    arrays = {
        "xq": np.ascontiguousarray(np.asarray(x).reshape(T, D)), "ctxT": ctxT, "mask": mask,
        "wqT": tr(L0_xattn_Wq), "wkT": tr(L0_xattn_Wk), "wvT": tr(L0_xattn_Wv), "woT": tr(L0_xattn_Wo),
        "bq": cols(L0_xattn_bq), "bk": cols(L0_xattn_bk),
        "bv": np.ascontiguousarray(np.asarray(L0_xattn_bv).reshape(KC, 2, 64).transpose(2, 0, 1)),
        "bo": np.asarray(L0_xattn_bo),
        "aqT": tr(L0_attn_Wq), "akT": tr(L0_attn_Wk), "avT": tr(L0_attn_Wv), "aoT": tr(L0_attn_Wo),
        "gw": np.ascontiguousarray(np.tile(np.asarray(L0_attn_gate_w), P // HD).reshape(P, 1)),
        "f1": np.asarray(L0_ffn_weight), "f2": np.asarray(L0_ffn_aux_weight1), "f3": np.asarray(L0_ffn_aux_weight2),
        "fb": np.asarray(L0_ffn_bias), "cosT": cosT, "sinT": sinT,
    }
    nc = bacc.Bacc("TRN2", target_bir_lowering=False, num_devices=1)
    args = [nc.dram_tensor(n, a.shape, mybir.dt.from_np(a.dtype), kind="ExternalInput").ap() for n, a in arrays.items()]
    out = nc.dram_tensor("out", (T, D), F32, kind="ExternalOutput").ap()
    build(nc, *args, out)
    r = run_bass_kernel_spmd(nc, [arrays], core_ids=[0])
    return r.results[0]["out"].reshape(B, LQ, D)
```

```python
from contextlib import ExitStack

import concourse.bass as bass
import numpy as np
from concourse import mybir

F32 = mybir.dt.float32
F32R = mybir.dt.float32r
BF16 = mybir.dt.bfloat16
F16 = mybir.dt.float16
U8 = mybir.dt.uint8
ALU = mybir.AluOpType
ACT = mybir.ActivationFunctionType
AX = mybir.AxisListType

P = 128
B, LQ, D = 8, 64, 512
S2, S2P = 1601, 1602
H, HD = 16, 32
KC = D // P
T = B * LQ
M = T // P
EPS = 1e-5
XSCALE = HD ** -0.5
FILL = -10000.0

CH = [(0, 384), (384, 384), (768, 384), (1152, 450)]
NT = -(-S2 // P)
ROWS = [min(P, S2 - P * t) for t in range(NT)]
CHUNK_END = [3, 6, 9, 13]
PAIRS = 4
VRING, PTRING = 8, 3

SLOTS = 20
T_LAG, PV_LAG = 5, 7
K_SEQ = [(c, j) for c in range(4) for j in range(2)]
K_SLOT = [dict(zip((4, 5, 9, 12, 14, 15, 17, 19), K_SEQ)), dict(zip((6, 7, 10, 12, 14, 15, 18, 19), K_SEQ))]
XH_SLOT = {3: 0, 6: 1, 9: 2, 13: 3}
V_PIECE, K_PIECE = [{}, {}], [{}, {}]
PIECES = [[], []]
for _h in range(2):
    for _s in range(SLOTS):
        if _s < NT:
            V_PIECE[_h][_s] = len(PIECES[_h])
            PIECES[_h].append(("v", _s))
        if _s in K_SLOT[_h]:
            K_PIECE[_h][K_SLOT[_h][_s]] = len(PIECES[_h])
            PIECES[_h].append(("k", K_SLOT[_h][_s]))
UNIT_PIECES = NT + 8
FIRST_PIECES = 8


SC_RING = 3


def pj_bank(i):
    return (FIRST_PIECES + i) % 3


def last_with(n, r, ring):
    return max(i for i in range(n) if i % ring == r)


def build(nc, xq, ctxT, mask, wqT, wkT, wvT, woT, bq, bk, bv, bo,
          aqT, akT, avT, aoT, gw, f1, f2, f3, fb, cosT, sinT, out):
    attn_dram = nc.dram_tensor("attn_scratch", (KC, P, B, LQ), F32).ap()
    base, loop, pro = ExitStack(), ExitStack(), ExitStack()

    def sb(ctx, name, shape, dt=F32):
        return ctx.enter_context(nc.sbuf_tensor(name, shape, dt))

    def sem(name):
        return base.enter_context(nc.semaphore(name))

    ident = sb(base, "ident", [P, P])
    gate = sb(base, "gate", [P, M])
    half_neg = sb(base, "half_neg", [P, M])
    bank = [base.enter_context(nc.psum_tensor(f"bank{i}", [P, 512], F32)) for i in range(8)]

    wk_h = sb(loop, "wk_h", [P, KC, D], F32R)
    wk_l = sb(loop, "wk_l", [P, KC, D], F32R)
    wv_h = sb(loop, "wv_h", [P, KC, D], F32R)
    wv_l = sb(loop, "wv_l", [P, KC, D], F32R)
    x_h = sb(loop, "x_h", [P, KC, S2P], F32R)
    x_l = sb(loop, "x_l", [P, KC, S2P], F32R)
    x_raw = sb(loop, "x_raw", [P, KC, 450])
    mask_u8 = sb(loop, "mask_u8", [P, S2P], U8)
    mask_f = sb(loop, "mask_f", [P, S2P], BF16)
    mask_b = sb(loop, "mask_b", [P, S2P], F16)
    bq_s = sb(loop, "bq_s", [P, KC])
    bk_s = sb(loop, "bk_s", [P, KC])
    bv_s = sb(loop, "bv_s", [64, KC, 2])
    qT = sb(loop, "qT", [P, 2, KC, T], F32R)
    q_bd = sb(loop, "q_bd", [P, PAIRS, 2, P], F32R)
    ks = sb(loop, "ks", [P, PAIRS, S2P], F32R)
    kf = sb(loop, "kf", [P, 2, 450])
    pt = sb(loop, "pt", [P, PTRING, PAIRS, 2, P], F32R)
    o_sb = sb(loop, "o_sb", [P, 2, 2, 2, P])
    o_fin = sb(loop, "o_fin", [64, 2, 2, P])
    o_out = sb(loop, "o_out", [P, 2, 2, LQ])
    smax = sb(loop, "smax", [P, PAIRS, 4])
    nmax = sb(loop, "nmax", [P, PAIRS])
    rsum = sb(loop, "rsum", [P, PAIRS])
    rinv = sb(loop, "rinv", [P, 2, PAIRS])

    xs0 = sb(pro, "xs0", [P, M, D])
    xT0 = sb(pro, "xT0", [P, KC, T])
    w_raw = sb(pro, "w_raw", [P, KC, D])
    st0 = sb(pro, "st0", [P, M, 6])
    mv0 = sb(pro, "mv0", [P, M, 2])
    ve0 = sb(pro, "ve0", [P, M])
    rs0 = sb(pro, "rs0", [P, M])
    gate_u8 = sb(pro, "gate_u8", [P, M, S2], U8)
    q_tmp = sb(pro, "q_tmp", [P, T])
    pro.close()
    prob = sb(loop, "prob", [P, PAIRS, S2])
    v = sb(loop, "v", [P, VRING, PAIRS, 2, 64], F32R)
    loop.close()

    tail = ExitStack()
    bo_s = sb(tail, "bo_s", [P, D])
    fb_s = sb(tail, "fb_s", [P, D])
    cos_s = sb(tail, "cos_s", [P, D])
    sin_s = sb(tail, "sin_s", [P, D])
    gw_s = sb(tail, "gw_s", [P, 1])
    w = [sb(tail, f"w{i}", [P, KC, D]) for i in range(8)]
    aT = sb(tail, "aT", [P, KC, T])
    x1 = sb(tail, "x1", [P, M, D])
    xn = sb(tail, "xn", [P, M, D])
    xT = sb(tail, "xT", [P, KC, T])
    st1 = sb(tail, "st1", [P, M, 6])
    mv1 = sb(tail, "mv1", [P, M, 2])
    ve1 = sb(tail, "ve1", [P, M])
    rs1 = sb(tail, "rs1", [P, M])
    y_s = sb(tail, "y_s", [P, 2, D])
    qk = sb(tail, "qk", [P, 2, D])
    v_t = sb(tail, "v_t", [P, M, D])
    rot = sb(tail, "rot", [P, 2, D])
    feat = sb(tail, "feat", [P, 2, H, 2, HD])
    featT = sb(tail, "featT", [P, 2, 8, P])
    sc = sb(tail, "sc", [P, H, LQ])
    mx = sb(tail, "mx", [P, H])
    sm = sb(tail, "sm", [P, H])
    ri = sb(tail, "ri", [P, H])
    pb = sb(tail, "pb", [P, H, P])
    pbT = sb(tail, "pbT", [P, H, P])
    o_t = sb(tail, "o_t", [P, KC, P])
    o_q = sb(tail, "o_q", [P, KC, P])
    tail.close()

    ident_ok = sem("ident_ok")
    small_in, xq_in, wq_in, wk_in, wv_in = sem("small_in"), sem("xq_in"), sem("wq_in"), sem("wk_in"), sem("wv_in")
    raw_in = [sem(f"raw_in{k}") for k in range(KC)]
    mask_in = sem("mask_in")
    ln_stat, ln_pow, ln_done = sem("ln_stat"), sem("ln_pow"), sem("ln_done")
    pro_mm, pro_ev, q_step, q_done = sem("pro_mm"), sem("pro_ev"), sem("q_step"), sem("q_done")
    w_hi, w_lo = sem("w_hi"), sem("w_lo")
    gate_in, gate_ok = sem("gate_in"), sem("gate_ok")
    x_hi, x_lo = sem("x_hi"), sem("x_lo")
    mask_ok, bias_ok = sem("mask_ok"), sem("bias_ok")
    qbd_zero, qbd_ok = sem("qbd_zero"), sem("qbd_ok")
    pj_done, v_lo = sem("pj_done"), sem("v_lo")
    kf_ok, k_hi, k_lo = sem("kf_ok"), sem("k_hi"), sem("k_lo")
    sc_done, sc_free, nmax_ok = sem("sc_done"), sem("sc_free"), sem("nmax_ok")
    exp_ok, rinv_ok, rb_done, o_scale = sem("exp_ok"), sem("rinv_ok"), sem("rb_done"), sem("o_scale")
    v_hi = sem("v_hi")
    t_done, t_hi, t_lo = sem("t_done"), sem("t_hi"), sem("t_lo")
    pv_done = sem("pv_done")
    o_copy, o_add, o_shift, o_comb, o_ready = (sem("o_copy"), sem("o_add"), sem("o_shift"), sem("o_comb"),
                                               sem("o_ready"))
    o_stored = [sem("o_stored0"), sem("o_stored1")]
    t_in = sem("t_in")
    tw_in = [sem(f"tw_in{i}") for i in range(8)]
    at_in = sem("at_in")
    mm, ev = sem("mm"), sem("ev")
    t_stat, t_pow, t_norm = sem("t_stat"), sem("t_pow"), sem("t_norm")
    rope, feat_ok = sem("rope"), sem("feat_ok")
    caus, s_sub, s_exp, s_sum, pb_zero, pb_ok = (sem("caus"), sem("s_sub"), sem("s_exp"), sem("s_sum"),
                                                 sem("pb_zero"), sem("pb_ok"))
    y_bias, o_sq, a2_ok = sem("y_bias"), sem("o_sq"), sem("a2_ok")
    res1, res2, pre_tanh, tanh_ok, res3 = (sem("res1"), sem("res2"), sem("pre_tanh"), sem("tanh_ok"), sem("res3"))
    out_done = sem("out_done")

    def wait(eng, s, n):
        if isinstance(n, int) and n <= 0:
            return
        eng.wait_ge(s, n)

    def wait_apart(eng, *counts):
        counts = [(sm_, n if isinstance(n, int) else eng.to_reg(n)) for sm_, n in counts]
        eng.wait_ge(ident_ok, 2)
        for sm_, n in counts:
            wait(eng, sm_, n)

    def piece_base(u):
        return u * UNIT_PIECES + FIRST_PIECES

    def batches(eng, unit):
        unit(0, 0, False)
        unit(0, 1, False)
        with eng.Fori(1, B - 1) as b:
            unit(b, 0, False)
            unit(b, 1, False)
        unit(B - 1, 0, False)
        unit(B - 1, 1, True)

    J_Y1, J_T1, J_ATT = 0, M, 2 * M
    J_Y2 = J_ATT + 16 * M
    J_T2 = J_Y2 + M
    J_F1 = J_T2 + M
    J_F2, J_F3 = J_F1 + KC, J_F1 + 2 * KC

    def job(kind, m, i=0):
        return J_ATT + 16 * m + {"qkv": 0, "feat": 3, "score": 7, "prob": 11, "o": 15}[kind] + i

    block = base.enter_context(nc.Block())

    @block.sync
    def _(sp):
        sp.dma_start(xs0[:], xq.rearrange("(m p) d -> p m d", p=P)).then_inc(xq_in, 16)
        for dst, src in ((bq_s, bq), (bk_s, bk), (bv_s, bv)):
            sp.dma_start(dst[:], src).then_inc(small_in, 16)
        sp.dma_start(w_raw[:], wqT.rearrange("(k p) n -> p k n", p=P)).then_inc(wq_in, 16)

        def load_chunk(b, c):
            c0, n = CH[c]
            for k in range(KC):
                wait_apart(sp, (x_lo, (b * 4 + c - 1) * KC + k + 1))
                sp.dma_start(x_raw[:, k, 0:n], ctxT[b, k * P:(k + 1) * P, c0:c0 + n]).then_inc(raw_in[k], 16)

        def load_mask(b):
            wait_apart(sp, (bias_ok, b))
            sp.dma_start(mask_u8[:], mask[b].partition_broadcast(P)).then_inc(mask_in, 16)

        load_chunk(0, 0)
        load_mask(0)
        for b in range(B):
            sp.dma_start(gate_u8[64 * (b % 2):64 * (b % 2) + 64, b // 2, :], mask[b, 0:S2].partition_broadcast(64))\
                .then_inc(gate_in, 16)
        sp.wait_ge(pro_mm, M + KC)
        sp.dma_start(w_raw[:], wkT.rearrange("(k p) n -> p k n", p=P)).then_inc(wk_in, 16)
        sp.wait_ge(w_lo, 1)
        sp.dma_start(w_raw[:], wvT.rearrange("(k p) n -> p k n", p=P)).then_inc(wv_in, 16)
        for c in range(1, 4):
            load_chunk(0, c)

        def store(b, h):
            sp.dma_start(attn_dram[2 * h:2 * h + 2, :, b, :].rearrange("g p q -> p g q"), o_out[:, h, :, :])\
                .then_inc(o_stored[h], 16)

        def unit(b, h, last):
            u = b * 2 + h
            if h == 1 and not last:
                load_mask(b + 1)
                load_chunk(b + 1, 0)
                load_chunk(b + 1, 1)
            if h == 1:
                wait_apart(sp, (o_ready, u))
                store(b, 0)
            elif not (isinstance(b, int) and b == 0):
                wait_apart(sp, (o_ready, u))
                store(b - 1, 1)
            if h == 1 and not last:
                load_chunk(b + 1, 2)
                load_chunk(b + 1, 3)

        batches(sp, unit)
        sp.wait_ge(o_ready, 2 * B)
        store(B - 1, 1)
        sp.wait_ge(o_stored[0], 16 * B)
        sp.wait_ge(o_stored[1], 16 * B)
        sp.dma_start(aT[:], attn_dram.rearrange("k p b q -> p k (b q)")).then_inc(at_in, 16)
        order = (woT, aqT, akT, avT, aoT, f1, f2, f3)
        sp.dma_start(w[0][:], order[0].rearrange("(k p) n -> p k n", p=P)).then_inc(tw_in[0], 16)
        sp.dma_start(x1[:], xq.rearrange("(m p) d -> p m d", p=P)).then_inc(t_in, 16)
        sp.dma_start(bo_s[:], bo.partition_broadcast(P)).then_inc(t_in, 16)
        sp.dma_start(fb_s[:], fb.partition_broadcast(P)).then_inc(t_in, 16)
        sp.dma_start(cos_s[:], cosT).then_inc(t_in, 16)
        sp.dma_start(sin_s[:], sinT).then_inc(t_in, 16)
        sp.dma_start(gw_s[:], gw).then_inc(t_in, 16)
        for i in range(1, 8):
            sp.dma_start(w[i][:], order[i].rearrange("(k p) n -> p k n", p=P)).then_inc(tw_in[i], 16)
        for m in range(M):
            sp.wait_ge(res3, m + 1)
            sp.dma_start(out[m * P:(m + 1) * P, :], x1[:, m, :]).then_inc(out_done, 16)
        sp.wait_ge(out_done, 16 * M)

    @block.gpsimd
    def _(pool):
        pool.memset(ident[:], 0.0).then_inc(ident_ok, 1)
        pool.wait_ge(ident_ok, 1)
        pool.affine_select(out=ident[:], in_=ident[:], compare_op=ALU.not_equal, fill=1.0, base=0,
                           pattern=[[-1, P]], channel_multiplier=1).then_inc(ident_ok, 1)
        pool.memset(half_neg[:], -0.5).then_inc(ln_pow, 1)
        pool.memset(q_bd[:].bitcast(F32), 0.0).then_inc(qbd_zero, 1)
        pool.wait_ge(ln_pow, 1)
        for m in range(M):
            pool.wait_ge(ln_stat, 3 * m + 3)
            pool.tensor_tensor(rs0[:, m:m + 1], ve0[:, m:m + 1], half_neg[:, m:m + 1], ALU.pow).then_inc(ln_pow, 1)

        def split_chunk(b, c):
            c0, n = CH[c]
            for k in range(KC):
                pool.wait_ge(x_hi, (b * 4 + c) * KC + k + 1)
                pool.tensor_tensor(x_l[:, k, c0:c0 + n], x_raw[:, k, 0:n], x_h[:, k, c0:c0 + n].bitcast(F32),
                                   ALU.subtract).then_inc(x_lo, 1)

        def make_mask(b):
            wait_apart(pool, (mask_in, b * 16 + 16), (kf_ok, b * 16))
            pool.tensor_copy(mask_f[:], mask_u8[:]).then_inc(mask_ok, 1)

        def make_bias(b):
            wait_apart(pool, (sc_free, b * 32), (mask_ok, b + 1))
            pool.tensor_scalar(mask_b[:], mask_f[:], -FILL, FILL, ALU.mult, ALU.add).then_inc(bias_ok, 1)

        split_chunk(0, 0)
        make_mask(0)
        make_bias(0)
        for c in range(1, 4):
            split_chunk(0, c)

        def unit(b, h, last):
            if h == 1 and not last:
                make_mask(b + 1)
                make_bias(b + 1)
                for c in range(4):
                    split_chunk(b + 1, c)

        batches(pool, unit)

        def inv_std(n):
            for m in range(M):
                pool.wait_ge(t_stat, n * 3 * M + 3 * m + 3)
                pool.tensor_tensor(rs1[:, m:m + 1], ve1[:, m:m + 1], half_neg[:, m:m + 1], ALU.pow).then_inc(t_pow, 1)

        pool.wait_ge(at_in, 16)
        pool.memset(pb[:], 0.0).then_inc(pb_zero, 1)
        inv_std(0)
        for m in range(M):
            pool.wait_ge(ev, job("score", m, 3) + 1)
            for r in range(2):
                pool.affine_select(out=sc[64 * r:64 * r + 64], in_=sc[64 * r:64 * r + 64], compare_op=ALU.is_ge,
                                   fill=-1e9, base=0, pattern=[[0, H], [-1, LQ]], channel_multiplier=1)\
                    .then_inc(caus, 1)
        inv_std(1)

    @block.scalar
    def _(act):
        for m in range(M):
            act.wait_ge(pro_mm, m + 1)
            act.activation(xT0[:, :, m * P:(m + 1) * P], bank[4 + m][:].rearrange("p (k t) -> p k t", k=KC), ACT.Copy)\
                .then_inc(pro_ev, 1)

        def split_chunk(b, c):
            c0, n = CH[c]
            for k in range(KC):
                act.wait_ge(raw_in[k], (b * 4 + c) * 16 + 16)
                if not (isinstance(b, int) and b == 0):
                    act.wait_ge(pj_done, piece_base(b * 2 - 1) + V_PIECE[1][CHUNK_END[c] - 1] + 1)
                act.activation(x_h[:, k, c0:c0 + n], x_raw[:, k, 0:n], ACT.Copy).then_inc(x_hi, 1)

        split_chunk(0, 0)
        act.wait_ge(wk_in, 16)
        act.activation(wk_h[:], w_raw[:], ACT.Copy).then_inc(w_hi, 1)
        act.wait_ge(wv_in, 16)
        act.activation(wv_h[:], w_raw[:], ACT.Copy).then_inc(w_hi, 1)
        for c in range(1, 4):
            split_chunk(0, c)

        def q_blocks(b, h, u):
            wait(act, sc_done, u * 16)
            for r in range(4):
                for par in range(2):
                    src = 32 * (r % 2) + 64 * par
                    a = act.activation(
                        q_bd[32 * r:32 * r + 32, par::2, :, 64 * (r % 2):64 * (r % 2) + 64],
                        qT[src:src + 32, :, 2 * h:2 * h + 2, bass.ds(b * LQ, LQ)].bitcast(F32)
                        .rearrange("p l g q -> p g l q"), ACT.Copy)
            a.then_inc(qbd_ok, 1)

        def key_hi(n):
            c, j, count = n
            c0, w_ = CH[c]
            act.wait_ge(kf_ok, count + 1)
            sl = K_SEQ.index((c, j)) % 2
            act.activation(ks[0:64, 2 * j, c0:c0 + w_], kf[0:64, sl, 0:w_], ACT.Copy).then_inc(k_hi, 1)
            act.activation(ks[64:128, 2 * j + 1, c0:c0 + w_], kf[64:128, sl, 0:w_], ACT.Copy).then_inc(k_hi, 1)

        act.wait_ge(qbd_zero, 1)
        act.wait_ge(q_done, KC)
        q_blocks(0, 0, 0)
        for i, (c, j) in enumerate(K_SEQ):
            key_hi((c, j, i))

        def exp_pair(u, p):
            act.wait_ge(nmax_ok, u * PAIRS + p + 1)
            act.activation(prob[:, p, :], prob[:, p, :], ACT.Exp, bias=nmax[:, p:p + 1], scale=1.0,
                           accum_out=rsum[:, p:p + 1]).then_inc(exp_ok, 1)

        def out_copy(u):
            act.wait_ge(pv_done, (u + 1) * NT)
            wait(act, o_comb, u)
            for j in range(2):
                act.activation(o_sb[:, j].rearrange("p a l q -> p (a l q)"), bank[6 + j][:], ACT.Copy).then_inc(o_copy, 1)

        def out_shift(u):
            act.wait_ge(o_scale, u + 1)
            wait(act, o_ready, u)
            act.activation(o_fin[:], o_sb[64:128, :, :, 0, :], ACT.Copy).then_inc(o_shift, 1)

        def unit(b, h, last):
            u = b * 2 + h
            first = isinstance(b, int) and b == 0 and h == 0
            for s in range(SLOTS):
                if s < NT:
                    act.wait_ge(pj_done, piece_base(u) + (s if last else V_PIECE[h][s]) + 1)
                    prev = u * NT + s - VRING + 1 if s >= VRING else (u - 1) * NT + \
                        (s + VRING if s + VRING < NT else s) + 1
                    wait(act, pv_done, prev)
                    r = ROWS[s]
                    pj = bank[pj_bank(s if last else V_PIECE[h][s])]
                    act.activation(v[0:r, s % VRING, :, 0, :], pj[0:r, 0:256].rearrange("p (a d) -> p a d", a=PAIRS),
                                   ACT.Copy).then_inc(v_hi, 1)
                if s in XH_SLOT and h == 1 and not last:
                    split_chunk(b + 1, XH_SLOT[s])
                if s < 4:
                    exp_pair(u, s)
                if 0 <= s - T_LAG < NT:
                    t = s - T_LAG
                    r = ROWS[t]
                    act.wait_ge(t_done, u * NT + t + 1)
                    wait(act, pv_done, u * NT + t - PTRING + 1 if t >= PTRING else (u - 1) * NT +
                         last_with(NT, t, PTRING) + 1)
                    act.activation(pt[0:r, t % PTRING, :, 0, :], bank[3 + t % SC_RING][0:r, :].rearrange("p (a q) -> p a q", a=PAIRS),
                                   ACT.Copy).then_inc(t_hi, 1)
                if s in K_SLOT[h] and not last:
                    c, j = K_SLOT[h][s]
                    if (c, j) == (0, 0):
                        act.wait_ge(sc_done, (u + 1) * 16)
                    key_hi((c, j, (u + 1) * 8 + K_SEQ.index((c, j))))
                if s == 4 and not first:
                    out_copy(u - 1)
                if s == 6 and not first:
                    out_shift(u - 1)
                if s == 7 and not last:
                    if h == 0:
                        q_blocks(b, 1, u + 1)
                    else:
                        q_blocks(b + 1, 0, u + 1)

        batches(act, unit)
        out_copy(2 * B - 1)
        out_shift(2 * B - 1)

        act.wait_ge(at_in, 16)
        n_ev = [0]

        def take(dst, src):
            act.wait_ge(mm, n_ev[0] + 1)
            i = act.activation(dst, src, ACT.Copy)
            i.then_inc(ev, 1)
            n_ev[0] += 1

        def bk_of(n):
            return bank[n % 8]

        for m in range(M):
            if m >= 2:
                act.wait_ge(res1, m - 1)
            take(y_s[:, m % 2, :], bk_of(J_Y1 + m)[:])
        for m in range(M):
            take(xT[:, :, m * P:(m + 1) * P], bk_of(J_T1 + m)[:].rearrange("p (k t) -> p k t", k=KC))
        for m in range(M):
            for i in range(3):
                if i < 2 and m > 0:
                    act.wait_ge(rope, 6 * m)
                take(qk[:, i, :] if i < 2 else v_t[:, m, :], bk_of(job("qkv", m, i))[:])
            for f in range(2):
                for q4 in range(2):
                    take(featT[:, f, 4 * q4:4 * q4 + 4, :], bk_of(job("feat", m, 2 * f + q4))[:].rearrange("p (a t) -> p a t", a=4))
            if m > 0:
                act.wait_ge(pb_ok, 2 * m)
            for i in range(4):
                src = bk_of(job("score", m, i))[:].rearrange("p (a t) -> p a t", a=4)
                h0 = 8 * (i % 2) + i // 2
                act.wait_ge(mm, job("score", m, i) + 1)
                act.activation(sc[0:64, h0:h0 + 7:2, :], src[0:64, :, 0:64], ACT.Copy)
                act.activation(sc[64:128, h0:h0 + 7:2, :], src[64:128, :, 64:128], ACT.Copy).then_inc(ev, 1)
                n_ev[0] += 1
            act.wait_ge(s_sub, 2 * m + 2)
            act.activation(sc[:], sc[:], ACT.Exp).then_inc(s_exp, 1)
            for i in range(4):
                take(pbT[:, 4 * i:4 * i + 4, :], bk_of(job("prob", m, i))[:].rearrange("p (a t) -> p a t", a=4))
            if m > 0:
                act.wait_ge(a2_ok, m)
            take(o_t[:], bk_of(job("o", m))[:].rearrange("p (k t) -> p k t", k=KC))
        for m in range(M):
            if m >= 2:
                act.wait_ge(res2, m - 1)
            take(y_s[:, m % 2, :], bk_of(J_Y2 + m)[:])
        for m in range(M):
            take(xT[:, :, m * P:(m + 1) * P], bk_of(J_T2 + m)[:].rearrange("p (k t) -> p k t", k=KC))
        for g in range(KC):
            take(aT[:, g, :], bk_of(J_F1 + g)[:])
        act.wait_ge(mm, J_F2 + KC)
        for g in range(KC):
            take(xT[:, g, :], bk_of(J_F2 + g)[:])
        for m in range(M):
            take(xn[:, m, :], bk_of(J_F3 + m)[:])
        for m in range(M):
            act.wait_ge(pre_tanh, m + 1)
            act.activation(xn[:, m, :], xn[:, m, :], ACT.Tanh).then_inc(tanh_ok, 1)

    @block.vector
    def _(dve):
        for m in range(M):
            if m == 0:
                dve.wait_ge(xq_in, 16)
            dve.bn_stats(st0[:, m, :], xs0[:, m, :]).then_inc(ln_stat, 1)
            dve.wait_ge(ln_stat, 3 * m + 1)
            dve.bn_aggr(mv0[:, m, :], st0[:, m, :]).then_inc(ln_stat, 1)
            dve.wait_ge(ln_stat, 3 * m + 2)
            dve.tensor_scalar(ve0[:, m:m + 1], mv0[:, m, 1:2], EPS, None, ALU.add).then_inc(ln_stat, 1)
        for m in range(M):
            dve.wait_ge(ln_pow, m + 2)
            dve.tensor_scalar(xs0[:, m, :], xs0[:, m, :], mv0[:, m, 0:1], rs0[:, m:m + 1],
                              ALU.subtract, ALU.mult).then_inc(ln_done, 1)
        dve.wait_ge(small_in, 48)
        for g in range(KC):
            dve.wait_ge(pro_mm, M + g + 1)
            dve.tensor_scalar(q_tmp[:], bank[g][:], bq_s[:, g:g + 1], XSCALE, ALU.add, ALU.mult).then_inc(q_step, 1)
            dve.wait_ge(q_step, 2 * g + 1)
            dve.tensor_copy(qT[:, 0, g, :], q_tmp[:]).then_inc(q_step, 1)
            dve.wait_ge(q_step, 2 * g + 2)
            dve.tensor_tensor(qT[:, 1, g, :], q_tmp[:], qT[:, 0, g, :].bitcast(F32), ALU.subtract).then_inc(q_done, 1)
            dve.wait_ge(q_done, g + 1)
        dve.wait_ge(gate_in, 16 * B)
        dve.tensor_reduce(gate[:], gate_u8[:], AX.X, ALU.max).then_inc(gate_ok, 1)
        dve.wait_ge(w_hi, 1)
        dve.tensor_tensor(wk_l[:], w_raw[:], wk_h[:].bitcast(F32), ALU.subtract).then_inc(w_lo, 1)
        dve.wait_ge(w_hi, 2)
        dve.tensor_tensor(wv_l[:], w_raw[:], wv_h[:].bitcast(F32), ALU.subtract).then_inc(w_lo, 1)

        def key_full(c, j, count, piece, g, bk, b):
            c0, n = CH[c]
            dve.wait_ge(pj_done, piece + 1)
            sl = K_SEQ.index((c, j)) % 2
            if K_SEQ.index((c, j)) == 0:
                dve.wait_ge(mask_ok, b + 1)
            wait(dve, k_lo, 2 * (count - 1))
            dve.scalar_tensor_tensor(kf[:, sl, 0:n], bank[bk][:, 0:n], bk_s[:, g:g + 1], mask_f[:, c0:c0 + n],
                                     ALU.add, ALU.mult).then_inc(kf_ok, 1)

        def key_lo(c, j, count):
            c0, n = CH[c]
            sl = K_SEQ.index((c, j)) % 2
            dve.wait_ge(k_hi, 2 * count + 2)
            dve.tensor_tensor(ks[64:128, 2 * j, c0:c0 + n], kf[0:64, sl, 0:n], ks[0:64, 2 * j, c0:c0 + n].bitcast(F32),
                              ALU.subtract).then_inc(k_lo, 1)
            dve.tensor_tensor(ks[0:64, 2 * j + 1, c0:c0 + n], kf[64:128, sl, 0:n],
                              ks[64:128, 2 * j + 1, c0:c0 + n].bitcast(F32), ALU.subtract).then_inc(k_lo, 1)

        for i, (c, j) in enumerate(K_SEQ):
            key_full(c, j, i, i, j, i % 3, 0)
            if i < len(K_SEQ) - 1:
                key_lo(c, j, i)

        def score_chunk(u, p, c):
            if p == 0 and c == 0:
                wait(dve, t_done, u * NT)
            c0, n = CH[c]
            n = min(n, S2 - c0)
            wait_apart(dve, (sc_done, u * 16 + 4 * p + c + 1))
            dve.tensor_tensor_reduce(prob[:, p, c0:c0 + n], bank[3 + (4 * p + c) % SC_RING][:, 0:n], mask_b[:, c0:c0 + n],
                                     1.0, -3.0e38, ALU.add, ALU.max, smax[:, p, c:c + 1]).then_inc(sc_free, 1)

        def neg_max(u, p):
            dve.wait_ge(sc_free, u * 16 + 4 * p + 4)
            dve.tensor_reduce(nmax[:, p:p + 1], smax[:, p, :], AX.X, ALU.max, negate=True).then_inc(nmax_ok, 1)

        def recip(u, h, p):
            dve.wait_ge(exp_ok, u * PAIRS + p + 1)
            if p == 0:
                wait(dve, rb_done, u - 1)
            dve.reciprocal(rinv[:, h, p:p + 1], rsum[:, p:p + 1]).then_inc(rinv_ok, 1)

        def out_add(u):
            for j in range(2):
                dve.wait_ge(o_copy, u * 2 + j + 1)
                dve.tensor_tensor(o_sb[:, j, :, 0, :], o_sb[:, j, :, 0, :], o_sb[:, j, :, 1, :], ALU.add).then_inc(o_add, 1)
            dve.wait_ge(o_add, (u + 1) * 2)
            dve.wait_ge(rb_done, u + 1)
            dve.tensor_tensor(o_sb[:, :, :, 0, :], o_sb[:, :, :, 0, :],
                              bank[6][:].rearrange("p (j a q) -> p j a q", j=2, a=2), ALU.mult).then_inc(o_scale, 1)

        def out_combine(u, b, h):
            dve.wait_ge(o_shift, u + 1)
            dve.tensor_tensor(o_fin[:], o_sb[0:64, :, :, 0, :], o_fin[:], ALU.add).then_inc(o_comb, 1)
            dve.wait_ge(o_comb, u + 1)
            wait(dve, o_stored[h], b * 16)
            for a in range(2):
                for i in range(2):
                    for j in range(2):
                        r = 64 * a + 32 * i
                        g = 2 * h + j
                        op = dve.tensor_scalar(o_out[r:r + 32, h, j, :], o_fin[32 * i:32 * i + 32, j, a, 64 * i:64 * i + 64],
                                               bv_s[32 * i:32 * i + 32, g, a:a + 1], None, ALU.add)
            op.then_inc(o_ready, 1)

        def value_lo(u, h, s, last):
            dve.wait_ge(v_hi, u * NT + s + 1)
            r = ROWS[s]
            pj = bank[pj_bank(s if last else V_PIECE[h][s])]
            dve.tensor_tensor(v[0:r, s % VRING, :, 1, :], pj[0:r, 0:256].rearrange("p (a d) -> p a d", a=PAIRS),
                              v[0:r, s % VRING, :, 0, :].bitcast(F32), ALU.subtract).then_inc(v_lo, 1)

        def unit(b, h, last):
            u = b * 2 + h
            first = isinstance(b, int) and b == 0 and h == 0
            key_pending = None
            for s in range(SLOTS):
                if s < 4:
                    if s == 0 and h == 0:
                        dve.wait_ge(bias_ok, b + 1)
                    score_chunk(u, s, 0)
                    if s > 0:
                        value_lo(u, h, s - 1, last)
                    score_chunk(u, s, 1)
                    if s == 0:
                        key_lo(*K_SEQ[-1], u * 8 + 7)
                    score_chunk(u, s, 2)
                    score_chunk(u, s, 3)
                    neg_max(u, s)
                    if s > 0:
                        recip(u, h, s - 1)
                if s == 4:
                    value_lo(u, h, 3, last)
                if 4 <= s < NT:
                    value_lo(u, h, s, last)
                if s == 4:
                    recip(u, h, 3)
                if key_pending:
                    key_lo(*key_pending)
                    key_pending = None
                if s in K_SLOT[h] and not last:
                    c, j = K_SLOT[h][s]
                    nb, nh = (b, 1) if h == 0 else (b + 1, 0)
                    i = K_SEQ.index((c, j))
                    key_full(c, j, (u + 1) * 8 + i, piece_base(u) + K_PIECE[h][(c, j)], 2 * nh + j,
                             pj_bank(K_PIECE[h][(c, j)]), nb)
                    key_pending = (c, j, (u + 1) * 8 + i)
                if 0 <= s - T_LAG < NT:
                    t = s - T_LAG
                    r = ROWS[t]
                    dve.wait_ge(t_hi, u * NT + t + 1)
                    dve.tensor_tensor(pt[0:r, t % PTRING, :, 1, :], bank[3 + t % SC_RING][0:r, :].rearrange("p (a q) -> p a q", a=PAIRS),
                                      pt[0:r, t % PTRING, :, 0, :].bitcast(F32), ALU.subtract).then_inc(t_lo, 1)
                if s == 5 and not first:
                    out_add(u - 1)
                if s == 7 and not first:
                    out_combine(u - 1, b - 1 if h == 0 else b, 1 - h)

        batches(dve, unit)
        out_add(2 * B - 1)
        out_combine(2 * B - 1, B - 1, 1)

        dve.wait_ge(t_in, 16 * 6)

        def layer_norm(n):
            for m in range(M):
                c = n * 3 * M + 3 * m
                dve.bn_stats(st1[:, m, :], x1[:, m, :]).then_inc(t_stat, 1)
                dve.wait_ge(t_stat, c + 1)
                dve.bn_aggr(mv1[:, m, :], st1[:, m, :]).then_inc(t_stat, 1)
                dve.wait_ge(t_stat, c + 2)
                dve.tensor_scalar(ve1[:, m:m + 1], mv1[:, m, 1:2], EPS, None, ALU.add).then_inc(t_stat, 1)
            for m in range(M):
                dve.wait_ge(t_pow, n * M + m + 1)
                dve.tensor_scalar(xn[:, m, :], x1[:, m, :], mv1[:, m, 0:1], rs1[:, m:m + 1],
                                  ALU.subtract, ALU.mult).then_inc(t_norm, 1)

        dve.wait_ge(gate_ok, 1)
        for m in range(M):
            dve.wait_ge(ev, J_Y1 + m + 1)
            dve.tensor_tensor(y_s[:, m % 2, :], y_s[:, m % 2, :], bo_s[:], ALU.add).then_inc(y_bias, 1)
            dve.wait_ge(y_bias, m + 1)
            dve.scalar_tensor_tensor(x1[:, m, :], y_s[:, m % 2, :], gate[:, m:m + 1], x1[:, m, :],
                                     ALU.mult, ALU.add).then_inc(res1, 1)
            dve.wait_ge(res1, m + 1)
        layer_norm(0)
        q_scale = HD ** -0.5
        for m in range(M):
            for i in range(2):
                n = 6 * m + 3 * i
                dve.wait_ge(ev, job("qkv", m, i) + 1)
                src = qk[:, i, :].rearrange("p (h d) -> p h d", h=H)
                dst = rot[:, i, :].rearrange("p (h d) -> p h d", h=H)
                sn = sin_s[:].rearrange("p (h d) -> p h d", h=H)
                if m > 0 and i == 0:
                    dve.wait_ge(feat_ok, 4 * m)
                dve.tensor_tensor(dst[:, :, 0:16], src[:, :, 16:32], sn[:, :, 0:16], ALU.mult)
                dve.tensor_tensor(dst[:, :, 16:32], src[:, :, 0:16], sn[:, :, 16:32], ALU.mult).then_inc(rope, 1)
                dve.wait_ge(rope, n + 1)
                dve.tensor_tensor(qk[:, i, :], qk[:, i, :], cos_s[:], ALU.mult).then_inc(rope, 1)
                dve.wait_ge(rope, n + 2)
                dve.tensor_tensor(rot[:, i, :], rot[:, i, :], qk[:, i, :], ALU.add).then_inc(rope, 1)
                dve.wait_ge(rope, n + 3)
                if m > 0:
                    dve.wait_ge(mm, job("feat", m - 1, 3) + 1)
                one, two = (q_scale, 0.1 * q_scale) if i == 0 else (1.0, 1.0)
                dve.tensor_scalar(feat[:, i, :, 0, :], dst, one, None, ALU.mult).then_inc(feat_ok, 1)
                dve.scalar_tensor_tensor(feat[:, i, :, 1, :], dst, two, dst, ALU.mult, ALU.mult).then_inc(feat_ok, 1)
            dve.wait_ge(caus, 2 * m + 2)
            dve.tensor_reduce(mx[:], sc[:], AX.X, ALU.max).then_inc(s_sub, 1)
            dve.wait_ge(s_sub, 2 * m + 1)
            dve.tensor_tensor(sc[:], sc[:], mx[:].unsqueeze(2).to_broadcast([P, H, LQ]), ALU.subtract).then_inc(s_sub, 1)
            dve.wait_ge(s_exp, m + 1)
            dve.tensor_reduce(sm[:], sc[:], AX.X, ALU.add).then_inc(s_sum, 1)
            dve.wait_ge(s_sum, 2 * m + 1)
            dve.reciprocal(ri[:], sm[:]).then_inc(s_sum, 1)
            dve.wait_ge(s_sum, 2 * m + 2)
            if m == 0:
                dve.wait_ge(pb_zero, 1)
            else:
                dve.wait_ge(mm, job("prob", m - 1, 3) + 1)
            for r in range(2):
                rr = slice(64 * r, 64 * r + 64)
                dve.tensor_tensor(pb[rr, :, 64 * r:64 * r + 64], sc[rr], ri[rr].unsqueeze(2).to_broadcast([64, H, LQ]),
                                  ALU.mult).then_inc(pb_ok, 1)
            dve.wait_ge(ev, job("o", m) + 1)
            dve.scalar_tensor_tensor(o_q[:], o_t[:], gw_s[:, 0:1], o_t[:], ALU.mult, ALU.mult).then_inc(o_sq, 1)
            dve.wait_ge(o_sq, m + 1)
            dve.scalar_tensor_tensor(aT[:, :, m * P:(m + 1) * P], o_q[:], 0.05, o_t[:], ALU.mult, ALU.add)\
                .then_inc(a2_ok, 1)
        for m in range(M):
            dve.wait_ge(ev, J_Y2 + m + 1)
            dve.tensor_tensor(x1[:, m, :], x1[:, m, :], y_s[:, m % 2, :], ALU.add).then_inc(res2, 1)
            dve.wait_ge(res2, m + 1)
        layer_norm(1)
        for m in range(M):
            dve.wait_ge(ev, J_F3 + m + 1)
            dve.tensor_tensor(xn[:, m, :], xn[:, m, :], fb_s[:], ALU.add).then_inc(pre_tanh, 1)
        for m in range(M):
            dve.wait_ge(tanh_ok, m + 1)
            dve.tensor_tensor(x1[:, m, :], x1[:, m, :], xn[:, m, :], ALU.add).then_inc(res3, 1)

    @block.tensor
    def _(pe):
        pe.wait_ge(ident_ok, 2)
        for m in range(M):
            pe.wait_ge(ln_done, m + 1)
            for k in range(KC):
                t = pe.transpose(bank[4 + m][:, k * P:(k + 1) * P], xs0[:, m, k * P:(k + 1) * P], ident[:])
            t.then_inc(pro_mm, 1)
        pe.wait_ge(pro_ev, M)
        pe.wait_ge(wq_in, 16)
        for g in range(KC):
            for k in range(KC):
                q = pe.matmul(bank[g][:], w_raw[:, k, g * P:(g + 1) * P], xT0[:, k, :], start=(k == 0), stop=(k == KC - 1))
            q.then_inc(pro_mm, 1)
        pe.wait_ge(q_done, KC)
        pe.wait_ge(w_lo, 1)

        def key_piece(c, j, b, h, bk):
            c0, n = CH[c]
            g = slice((2 * h + j) * P, (2 * h + j + 1) * P)
            if h == 0 and j == 0:
                pe.wait_ge(x_lo, b * 16 + 4 * (c + 1))
            passes = [(w_, x, k) for k in range(KC) for w_, x in ((wk_h, x_h), (wk_h, x_l), (wk_l, x_h))]
            for i, (w_, x, k) in enumerate(passes):
                mm_ = pe.matmul(bank[bk][:, 0:n], w_[:, k, g], x[:, k, c0:c0 + n],
                                start=(i == 0), stop=(i == len(passes) - 1))
            mm_.then_inc(pj_done, 1)

        for i, (c, j) in enumerate(K_SEQ):
            wait(pe, kf_ok, i - 2)
            key_piece(c, j, 0, 0, i % 3)
        pe.wait_ge(w_lo, 2)

        def bank_free(u, h, i, last):
            if i < 3:
                kind, what = PIECES[1 - h][UNIT_PIECES - 3 + i]
                if kind == "v":
                    wait(pe, v_lo, (u - 1) * NT + what + 1)
                else:
                    pe.wait_ge(kf_ok, u * 8 + K_SEQ.index(what) + 1)
            elif last:
                pe.wait_ge(v_lo, u * NT + i - 2)
            else:
                kind, what = PIECES[h][i - 3]
                if kind == "v":
                    pe.wait_ge(v_lo, u * NT + what + 1)
                else:
                    pe.wait_ge(kf_ok, (u + 1) * 8 + K_SEQ.index(what) + 1)

        def score_chunk(u, p, c):
            if p == 0 and c == 0:
                pe.wait_ge(qbd_ok, u + 1)
            c0, n = CH[c]
            i = 4 * p + c
            pe.wait_ge(k_lo, u * 16 + 2 * (2 * c + p // 2 + 1))
            if i < SC_RING:
                wait(pe, t_lo, (u - 1) * NT + last_with(NT, i, SC_RING) + 1)
            else:
                pe.wait_ge(sc_free, u * 16 + i - SC_RING + 1)
            for l in range(2):
                s_ = pe.matmul(bank[3 + i % SC_RING][:, 0:n], q_bd[:, p, 1 - l, :], ks[:, p, c0:c0 + n],
                               start=(l == 0), stop=(l == 1))
            s_.then_inc(sc_done, 1)

        def value_tile(u, h, s, last, parts=((0, 12),)):
            i = s if last else V_PIECE[h][s]
            bank_free(u, h, i, last)
            r = ROWS[s]
            t0 = s * P
            passes = [(x, w_, k) for k in range(KC) for x, w_ in ((x_h, wv_h), (x_h, wv_l), (x_l, wv_h))]
            for a, z in parts:
                for n in range(a, z):
                    x, w_, k = passes[n]
                    v_ = pe.matmul(bank[pj_bank(i)][0:r, 0:256], x[:, k, t0:t0 + r], w_[:, k, 256 * h:256 * h + 256],
                                   start=(n == 0), stop=(n == len(passes) - 1))
                if z == len(passes):
                    v_.then_inc(pj_done, 1)
                yield

        def turn_tile(u, t):
            r = ROWS[t]
            if t == 0:
                pe.wait_ge(exp_ok, (u + 1) * PAIRS)
            if t >= SC_RING:
                pe.wait_ge(t_lo, u * NT + t - SC_RING + 1)
            else:
                pe.wait_ge(sc_free, u * 16 + last_with(16, t, SC_RING) + 1)
            for p in range(PAIRS):
                t_ = pe.transpose(bank[3 + t % SC_RING][0:r, p * P:(p + 1) * P], prob[:, p, t * P:t * P + r], ident[:])
            t_.then_inc(t_done, 1)

        def product_tile(u, t):
            r = ROWS[t]
            if t == 0:
                wait(pe, o_scale, u)
            pe.wait_ge(v_lo, u * NT + t + 1)
            pe.wait_ge(t_lo, u * NT + t + 1)
            for p in range(PAIRS):
                o_ = pe.matmul(bank[6 + p // 2][:, 256 * (p % 2):256 * (p % 2) + 256], v[0:r, t % VRING, p, :, :],
                               pt[0:r, t % PTRING, p, :, :], start=(t == 0 and p % 2 == 0), stop=(t == NT - 1),
                               skip_group_check=True)
            o_.then_inc(pv_done, 1)

        def spread_scales(u, h):
            pe.wait_ge(o_copy, (u + 1) * 2)
            pe.wait_ge(rinv_ok, (u + 1) * PAIRS)
            for p in range(PAIRS):
                r_ = pe.matmul(bank[6][:, p * P:(p + 1) * P], rinv[:, h, p:p + 1].to_broadcast([P, P]), ident[:],
                               start=True, stop=True)
            r_.then_inc(rb_done, 1)

        def unit(b, h, last):
            u = b * 2 + h
            for s in range(SLOTS):
                if s < 4:
                    value = value_tile(u, h, s, last, ((0, 6), (6, 9), (9, 12)))
                    score_chunk(u, s, 0)
                    score_chunk(u, s, 1)
                    next(value)
                    score_chunk(u, s, 2)
                    next(value)
                    score_chunk(u, s, 3)
                    next(value)
                elif s < NT:
                    next(value_tile(u, h, s, last))
                if s in K_SLOT[h] and not last:
                    c, j = K_SLOT[h][s]
                    i = K_PIECE[h][(c, j)]
                    bank_free(u, h, i, last)
                    key_piece(c, j, b if h == 0 else b + 1, 1 - h, pj_bank(i))
                if 0 <= s - T_LAG < NT:
                    turn_tile(u, s - T_LAG)
                if 0 <= s - PV_LAG < NT:
                    product_tile(u, s - PV_LAG)
                if s == 5 and not (isinstance(b, int) and b == 0 and h == 0):
                    spread_scales(u - 1, 1 - h)

        batches(pe, unit)
        spread_scales(2 * B - 1, 1)

        n_mm = [0]

        def begin():
            if n_mm[0] >= 8:
                pe.wait_ge(ev, n_mm[0] - 7)
            return bank[n_mm[0] % 8]

        def done(i):
            i.then_inc(mm, 1)
            n_mm[0] += 1

        def rows_product(xt, wt, m):
            bk = begin()
            for k in range(KC):
                i = pe.matmul(bk[:], xt[:, k, m * P:(m + 1) * P], wt[:, k, :], start=(k == 0), stop=(k == KC - 1))
            done(i)

        def cols_product(wt, xt, g):
            bk = begin()
            for k in range(KC):
                i = pe.matmul(bk[:], wt[:, k, g * P:(g + 1) * P], xt[:, k, :], start=(k == 0), stop=(k == KC - 1))
            done(i)

        def turn4(src):
            bk = begin()
            for i in range(4):
                t_ = pe.transpose(bk[:, i * P:(i + 1) * P], src(i), ident[:])
            done(t_)

        pe.wait_ge(o_scale, 2 * B)
        pe.wait_ge(at_in, 16)
        pe.wait_ge(tw_in[0], 16)
        for m in range(M):
            rows_product(aT, w[0], m)
        for m in range(M):
            pe.wait_ge(t_norm, m + 1)
            turn4(lambda i: xn[:, m, i * P:(i + 1) * P])
        for m in range(M):
            pe.wait_ge(ev, J_T1 + m + 1)
            for i in range(3):
                pe.wait_ge(tw_in[1 + i], 16)
                rows_product(xT, w[1 + i], m)
            for f in range(2):
                pe.wait_ge(feat_ok, 4 * m + 2 * f + 2)
                flat = feat[:, f].rearrange("p h s d -> p (h s d)")
                for q4 in range(2):
                    turn4(lambda i: flat[:, (4 * q4 + i) * P:(4 * q4 + i + 1) * P])
            pe.wait_ge(ev, job("feat", m, 3) + 1)
            for i in range(4):
                bk = begin()
                r = 64 * (i // 2)
                for a in range(4):
                    hp = 4 * (i % 2) + a
                    s_ = pe.matmul(bk[:, a * P:(a + 1) * P], featT[r:r + 64, 0, hp, :], featT[r:r + 64, 1, hp, :],
                                   start=True, stop=True)
                done(s_)
            pe.wait_ge(pb_ok, 2 * m + 2)
            for i in range(4):
                turn4(lambda a: pb[:, 4 * i + a, :])
            pe.wait_ge(ev, job("prob", m, 3) + 1)
            bk = begin()
            for hd in range(H):
                r = 32 * (hd % 4)
                o_ = pe.matmul(bk[r:r + 32, (hd // 4) * P:(hd // 4 + 1) * P], v_t[:, m, HD * hd:HD * hd + HD], pbT[:, hd, :],
                               start=True, stop=True)
            done(o_)
        pe.wait_ge(tw_in[4], 16)
        for m in range(M):
            pe.wait_ge(a2_ok, m + 1)
            rows_product(aT, w[4], m)
        for m in range(M):
            pe.wait_ge(t_norm, M + m + 1)
            turn4(lambda i: xn[:, m, i * P:(i + 1) * P])
        pe.wait_ge(ev, J_T2 + M)
        pe.wait_ge(tw_in[5], 16)
        for g in range(KC):
            cols_product(w[5], xT, g)
        pe.wait_ge(ev, J_F1 + KC)
        pe.wait_ge(tw_in[6], 16)
        for g in range(KC):
            cols_product(w[6], aT, g)
        pe.wait_ge(ev, J_F2 + KC)
        pe.wait_ge(tw_in[7], 16)
        for m in range(M):
            rows_product(xT, w[7], m)

    base.close()
    return nc


def kernel(x, ctx_1024, mask_BxS2_bk1, L0_xattn_Wq, L0_xattn_bq, L0_xattn_Wk, L0_xattn_bk, L0_xattn_Wv, L0_xattn_bv,
           L0_xattn_Wo, L0_xattn_bo, L0_attn_Wq, L0_attn_Wk, L0_attn_Wv, L0_attn_Wo, L0_attn_gate_w, L0_ffn_weight,
           L0_ffn_aux_weight1, L0_ffn_aux_weight2, L0_ffn_bias):
    import concourse.bacc as bacc
    from concourse.bass_utils import run_bass_kernel_spmd

    def tr(a):
        return np.ascontiguousarray(np.asarray(a).T)

    def cols(a):
        return np.ascontiguousarray(np.asarray(a).reshape(KC, P).T)

    ctx = np.asarray(ctx_1024)
    ctxT = np.zeros((B, D, S2P), ctx.dtype)
    ctxT[:, :, :S2] = ctx.transpose(0, 2, 1)
    mask = np.zeros((B, S2P), bool)
    mask[:, :S2] = np.asarray(mask_BxS2_bk1)

    half = HD // 2
    inv = (1.0 / np.float32(10000.0) ** (np.arange(half, dtype=np.float32) / np.float32(half))).astype(np.float32)
    ang = (np.arange(LQ, dtype=np.float32)[:, None] * inv[None, :]).astype(np.float32)
    cos, sin = np.cos(ang).astype(np.float32), np.sin(ang).astype(np.float32)
    cosT = np.ascontiguousarray(np.tile(np.concatenate([cos, cos], 1), (P // LQ, H)))
    sinT = np.ascontiguousarray(np.tile(np.concatenate([-sin, sin], 1), (P // LQ, H)))

    arrays = {
        "xq": np.ascontiguousarray(np.asarray(x).reshape(T, D)), "ctxT": ctxT, "mask": mask,
        "wqT": tr(L0_xattn_Wq), "wkT": tr(L0_xattn_Wk), "wvT": tr(L0_xattn_Wv), "woT": tr(L0_xattn_Wo),
        "bq": cols(L0_xattn_bq), "bk": cols(L0_xattn_bk),
        "bv": np.ascontiguousarray(np.asarray(L0_xattn_bv).reshape(KC, 2, 64).transpose(2, 0, 1)),
        "bo": np.asarray(L0_xattn_bo),
        "aqT": tr(L0_attn_Wq), "akT": tr(L0_attn_Wk), "avT": tr(L0_attn_Wv), "aoT": tr(L0_attn_Wo),
        "gw": np.ascontiguousarray(np.tile(np.asarray(L0_attn_gate_w), P // HD).reshape(P, 1)),
        "f1": np.asarray(L0_ffn_weight), "f2": np.asarray(L0_ffn_aux_weight1), "f3": np.asarray(L0_ffn_aux_weight2),
        "fb": np.asarray(L0_ffn_bias), "cosT": cosT, "sinT": sinT,
    }
    nc = bacc.Bacc("TRN2", target_bir_lowering=False, num_devices=1)
    args = [nc.dram_tensor(n, a.shape, mybir.dt.from_np(a.dtype), kind="ExternalInput").ap() for n, a in arrays.items()]
    out = nc.dram_tensor("out", (T, D), F32, kind="ExternalOutput").ap()
    build(nc, *args, out)
    r = run_bass_kernel_spmd(nc, [arrays], core_ids=[0])
    return r.results[0]["out"].reshape(B, LQ, D)
```

```python
from contextlib import ExitStack

import concourse.bass as bass
import numpy as np
from concourse import mybir

F32 = mybir.dt.float32
F32R = mybir.dt.float32r
BF16 = mybir.dt.bfloat16
F16 = mybir.dt.float16
U8 = mybir.dt.uint8
ALU = mybir.AluOpType
ACT = mybir.ActivationFunctionType
AX = mybir.AxisListType

P = 128
B, LQ, D = 8, 64, 512
S2, S2P = 1601, 1602
H, HD = 16, 32
KC = D // P
T = B * LQ
M = T // P
EPS = 1e-5
XSCALE = HD ** -0.5
FILL = -10000.0

CH = [(0, 384), (384, 384), (768, 384), (1152, 450)]
NT = -(-S2 // P)
ROWS = [min(P, S2 - P * t) for t in range(NT)]
CHUNK_END = [3, 6, 9, 13]
PAIRS = 4
VRING, PTRING = 8, 3
GC = -(-S2 // (P // B))

SLOTS = 20
T_LAG, PV_LAG = 5, 7
K_SEQ = [(c, j) for c in range(4) for j in range(2)]
K_SLOT = [dict(zip((4, 5, 9, 12, 14, 15, 17, 19), K_SEQ)), dict(zip((6, 7, 10, 12, 14, 15, 18, 19), K_SEQ))]
XH_SLOT = {3: 0, 6: 1, 9: 2, 13: 3}
V_PIECE, K_PIECE = [{}, {}], [{}, {}]
PIECES = [[], []]
for _h in range(2):
    for _s in range(SLOTS):
        if _s < NT:
            V_PIECE[_h][_s] = len(PIECES[_h])
            PIECES[_h].append(("v", _s))
        if _s in K_SLOT[_h]:
            K_PIECE[_h][K_SLOT[_h][_s]] = len(PIECES[_h])
            PIECES[_h].append(("k", K_SLOT[_h][_s]))
UNIT_PIECES = NT + 8
FIRST_PIECES = 8


SC_RING = 3


def pj_bank(i):
    return (FIRST_PIECES + i) % 3


def last_with(n, r, ring):
    return max(i for i in range(n) if i % ring == r)


def build(nc, xq, ctxT, mask, wqT, wkT, wvT, woT, bq, bk, bv, bo,
          aqT, akT, avT, aoT, gw, f1, f2, f3, fb, cosT, sinT, mask_rows, batch_of, out):
    attn_dram = nc.dram_tensor("attn_scratch", (KC, P, B, LQ), F32).ap()
    base, loop, pro = ExitStack(), ExitStack(), ExitStack()

    def sb(ctx, name, shape, dt=F32):
        return ctx.enter_context(nc.sbuf_tensor(name, shape, dt))

    def sem(name):
        return base.enter_context(nc.semaphore(name))

    ident = sb(base, "ident", [P, P])
    gate = sb(base, "gate", [P, M])
    half_neg = sb(base, "half_neg", [P, M])
    bank = [base.enter_context(nc.psum_tensor(f"bank{i}", [P, 512], F32)) for i in range(8)]

    wk_h = sb(loop, "wk_h", [P, KC, D], F32R)
    wk_l = sb(loop, "wk_l", [P, KC, D], F32R)
    wv_h = sb(loop, "wv_h", [P, KC, D], F32R)
    wv_l = sb(loop, "wv_l", [P, KC, D], F32R)
    x_h = sb(loop, "x_h", [P, KC, S2P], F32R)
    x_l = sb(loop, "x_l", [P, KC, S2P], F32R)
    x_raw = sb(loop, "x_raw", [P, KC, 450])
    mask_u8 = sb(loop, "mask_u8", [P, S2P], U8)
    mask_f = sb(loop, "mask_f", [P, S2P], BF16)
    mask_b = sb(loop, "mask_b", [P, S2P], F16)
    bq_s = sb(loop, "bq_s", [P, KC])
    bk_s = sb(loop, "bk_s", [P, KC])
    bv_s = sb(loop, "bv_s", [64, KC, 2])
    qT = sb(loop, "qT", [P, 2, KC, T], F32R)
    q_bd = sb(loop, "q_bd", [P, PAIRS, 2, P], F32R)
    ks = sb(loop, "ks", [P, PAIRS, S2P], F32R)
    kf = sb(loop, "kf", [P, 2, 450])
    o_sb = sb(loop, "o_sb", [P, 2, 2, 2, P])
    o_fin = sb(loop, "o_fin", [64, 2, 2, P])
    o_out = sb(loop, "o_out", [P, 2, 2, LQ])
    smax = sb(loop, "smax", [P, PAIRS, 4])
    nmax = sb(loop, "nmax", [P, PAIRS])
    rsum = sb(loop, "rsum", [P, PAIRS])
    rinv = sb(loop, "rinv", [P, 2, PAIRS])

    xs0 = sb(pro, "xs0", [P, M, D])
    xT0 = sb(pro, "xT0", [P, KC, T])
    wq_raw = sb(pro, "wq_raw", [P, KC, D])
    wk_raw = sb(pro, "wk_raw", [P, KC, D])
    wv_raw = sb(pro, "wv_raw", [P, KC, D])
    st0 = sb(pro, "st0", [P, M, 6])
    mv0 = sb(pro, "mv0", [P, M, 2])
    ve0 = sb(pro, "ve0", [P, M])
    rs0 = sb(pro, "rs0", [P, M])
    gate_u8 = sb(pro, "gate_u8", [P, GC], U8)
    gate_part = sb(pro, "gate_part", [P, 2])
    batch_rows = sb(pro, "batch_rows", [P, T])
    q_tmp = sb(pro, "q_tmp", [P, T])
    pro.close()
    pt = sb(loop, "pt", [P, PTRING, PAIRS, 2, P], F32R)
    prob = sb(loop, "prob", [P, PAIRS, S2])
    v = sb(loop, "v", [P, VRING, PAIRS, 2, 64], F32R)
    loop.close()

    tail = ExitStack()
    pads = iter(range(9))

    def pad(nbytes):
        return sb(tail, f"pad{next(pads)}", [P, nbytes], U8)

    def raw_and_low(name):
        with ExitStack() as short:
            raw = sb(short, f"{name}_raw", [P, KC, D])
        return raw, sb(tail, f"{name}_l", [P, KC, D], F32R)

    w_r, w_l, w_h = [None] * 4, [None] * 4, [None] * 4
    for i in range(2):
        w_r[i], w_l[i] = raw_and_low(f"w{i}")
        w_h[i] = sb(tail, f"w_h{i}", [P, KC, D], F32R)
    aT_h = sb(tail, "aT_h", [P, KC, T], F32R)
    w_r[2], w_l[2] = raw_and_low("w2")
    w_h[2] = sb(tail, "w_h2", [P, KC, D], F32R)
    pad((KC * S2P - 6 * D * 2) * 4)
    w_r[3], w_l[3] = raw_and_low("w3")
    w_h[3] = sb(tail, "w_h3", [P, KC, D], F32R)
    cos_s = sb(tail, "cos_s", [P, D])
    sin_s = sb(tail, "sin_s", [P, D])
    bo_s = sb(tail, "bo_s", [P, D])
    fb_s = sb(tail, "fb_s", [P, D])
    pad((KC * S2P - 6 * D * 2) * 4)
    aT_r, aT_l = raw_and_low("aT")
    gw_s = sb(tail, "gw_s", [P, 1])
    pad(D * 4)
    o_t = sb(tail, "o_t", [P, KC, P])
    o_q = sb(tail, "o_q", [P, KC, P])
    pad(1060)
    x1 = sb(tail, "x1", [P, M, D])
    xn = sb(tail, "xn", [P, M, D])
    xT_h = sb(tail, "xT_h", [P, KC, T], F32R)
    xT_l = sb(tail, "xT_l", [P, KC, T], F32R)
    st1 = sb(tail, "st1", [P, M, 6])
    mv1 = sb(tail, "mv1", [P, M, 2])
    ve1 = sb(tail, "ve1", [P, M])
    rs1 = sb(tail, "rs1", [P, M])
    qk = sb(tail, "qk", [P, 2, D])
    v_t = sb(tail, "v_t", [P, M, D])
    rot_s = sb(tail, "rot_s", [P, 2, D])
    rot_c = sb(tail, "rot_c", [P, 2, D])
    feat = sb(tail, "feat", [P, 2, H, 2, HD])
    featT = sb(tail, "featT", [P, 2, 8, P])
    causal = sb(tail, "causal", [P, LQ])
    sc = sb(tail, "sc", [P, H, LQ])
    mx = sb(tail, "mx", [P, H])
    e_sum = sb(tail, "e_sum", [P, H])
    e_inv = sb(tail, "e_inv", [P, H])
    e_rows = sb(tail, "e_rows", [P, D])
    pb = sb(tail, "pb", [P, H, P])
    pbT = sb(tail, "pbT", [P, H, P])
    tail.close()

    ident_ok = sem("ident_ok")
    small_in, xq_in, wq_in, wk_in, wv_in = sem("small_in"), sem("xq_in"), sem("wq_in"), sem("wk_in"), sem("wv_in")
    raw_in = [sem(f"raw_in{k}") for k in range(KC)]
    mask_in = sem("mask_in")
    ln_stat, ln_pow, ln_done = sem("ln_stat"), sem("ln_pow"), sem("ln_done")
    pro_mm, pro_ev, q_step, q_done = sem("pro_mm"), sem("pro_ev"), sem("q_step"), sem("q_done")
    w_hi, w_lo = sem("w_hi"), sem("w_lo")
    gate_in, gate_ok = sem("gate_in"), sem("gate_ok")
    x_hi, x_lo = sem("x_hi"), [sem(f"x_lo{k}") for k in range(KC)]
    mask_ok, bias_ok = sem("mask_ok"), sem("bias_ok")
    qbd_zero, qbd_ok = sem("qbd_zero"), sem("qbd_ok")
    pj_done, v_lo = sem("pj_done"), sem("v_lo")
    kf_ok, k_hi, k_lo = sem("kf_ok"), sem("k_hi"), sem("k_lo")
    sc_done, sc_free, nmax_ok = sem("sc_done"), sem("sc_free"), sem("nmax_ok")
    exp_ok, rinv_ok, rb_done, o_scale = sem("exp_ok"), sem("rinv_ok"), sem("rb_done"), sem("o_scale")
    v_hi = sem("v_hi")
    t_done, t_hi, t_lo = sem("t_done"), sem("t_hi"), sem("t_lo")
    pv_done = sem("pv_done")
    o_copy, o_add, o_shift, o_comb, o_ready = (sem("o_copy"), sem("o_add"), sem("o_shift"), sem("o_comb"),
                                               sem("o_ready"))
    o_stored = [sem("o_stored0"), sem("o_stored1")]
    t_in, rot_in, gw_in = sem("t_in"), sem("rot_in"), sem("gw_in")
    tw_in = [sem(f"tw_in{i}") for i in range(8)]
    at_in = sem("at_in")
    mm, ev_a, ev_v, ev_low = sem("mm"), sem("ev_a"), sem("ev_v"), sem("ev_low")
    t_stat, t_pow, t_norm = sem("t_stat"), sem("t_pow"), sem("t_norm")
    sin_ok, cos_ok, feat_ok = sem("sin_ok"), sem("cos_ok"), sem("feat_ok")
    causal_ok, s_max, s_sub, s_exp, pb_zero = (sem("causal_ok"), sem("s_max"), sem("s_sub"), sem("s_exp"),
                                               sem("pb_zero"))
    s_sum, o_step = sem("s_sum"), sem("o_step")
    tw_hi, tw_lo = sem("tw_hi"), [sem(f"tw_lo{i}") for i in range(8)]
    at_hi, at_lo, split_hi = sem("at_hi"), sem("at_lo"), sem("split_hi")
    bo_add, tanh_ok, res3 = sem("bo_add"), sem("tanh_ok"), sem("res3")
    out_done = sem("out_done")

    def wait(eng, s, n):
        if isinstance(n, int) and n <= 0:
            return
        eng.wait_ge(s, n)

    def wait_apart(eng, *counts):
        counts = [(sm_, n if isinstance(n, int) else eng.to_reg(n)) for sm_, n in counts]
        eng.wait_ge(ident_ok, 2)
        for sm_, n in counts:
            wait(eng, sm_, n)

    def piece_base(u):
        return u * UNIT_PIECES + FIRST_PIECES

    def batches(eng, unit):
        unit(0, 0, False)
        unit(0, 1, False)
        with eng.Fori(1, B - 1) as b:
            unit(b, 0, False)
            unit(b, 1, False)
        unit(B - 1, 0, False)
        unit(B - 1, 1, True)

    JOBS = [("y1", 0, 0), ("y1", 1, 0), ("y1", 2, 0), ("t1", 0, 0), ("y1", 3, 0)]
    JOBS += [("qkv", 0, i) for i in range(3)] + [("t1", 1, 0)]
    for m in range(M - 1):
        JOBS += [("feat", m, i) for i in range(4)] + [("score", m, i) for i in range(4)]
        JOBS += [("qkv", m + 1, i) for i in range(3)] + ([("t1", m + 2, 0)] if m < M - 2 else [])
        JOBS += [("prob", m, i) for i in range(4)] + [("o", m, 0), ("den", m, 0)]
    JOBS += [("feat", 3, i) for i in range(4)] + [("score", 3, i) for i in range(4)]
    JOBS += [("y2", 0, 0), ("y2", 1, 0), ("y2", 2, 0)] + [("prob", 3, i) for i in range(4)]
    JOBS += [("t2", 0, 0), ("o", 3, 0), ("den", 3, 0), ("t2", 1, 0), ("f1", 0, 0), ("f1", 0, 1), ("t2", 2, 0), ("y2", 3, 0),
             ("f2", 0, 0), ("t2", 3, 0), ("f2", 0, 1), ("f1", 1, 0), ("f1", 1, 1), ("f3", 0, 0),
             ("f2", 1, 0), ("f2", 1, 1), ("f3", 1, 0), ("f3", 2, 0), ("f3", 3, 0)]
    BY_VECTOR = ("y1", "score", "den", "y2", "f3")
    SPLIT = [j for j in JOBS if j[0] in ("t1", "t2", "f1", "f2")]
    BY_SCALAR = ("qkv", "feat", "prob", "o")
    AT_SELF = M

    def job(kind, m, i=0):
        return JOBS.index((kind, m, i))

    def bank_of(kind, m, i=0):
        return bank[job(kind, m, i) % 8]

    def computed(eng, kind, m, i=0):
        eng.wait_ge(mm, job(kind, m, i) + 1)

    def emptied(eng, kind, m, i=0):
        if (kind, m, i) in SPLIT:
            eng.wait_ge(ev_low, SPLIT.index((kind, m, i)) + 1)
            return
        kinds, s_ = (BY_VECTOR, ev_v) if kind in BY_VECTOR else (BY_SCALAR, ev_a)
        eng.wait_ge(s_, sum(j[0] in kinds for j in JOBS[:job(kind, m, i) + 1]))

    block = base.enter_context(nc.Block())

    @block.sync
    def _(sp):
        def load_chunk(b, c):
            c0, n = CH[c]
            for k in range(KC):
                wait_apart(sp, (x_lo[k], b * 4 + c))
                sp.dma_start(x_raw[:, k, 0:n], ctxT[b, k * P:(k + 1) * P, c0:c0 + n]).then_inc(raw_in[k], 16)

        def load_mask(b):
            wait_apart(sp, (bias_ok, b))
            sp.dma_start(mask_u8[:], mask[b].partition_broadcast(P)).then_inc(mask_in, 16)

        def load_raw(dst, src, s_):
            sp.dma_start(dst[:], src.rearrange("(k p) n -> p k n", p=P)).then_inc(s_, 16)

        load_mask(0)
        load_chunk(0, 0)
        load_raw(wk_raw, wkT, wk_in)
        load_raw(xs0, xq, xq_in)
        load_chunk(0, 1)
        for dst, src in ((bq_s, bq), (bk_s, bk), (bv_s, bv)):
            sp.dma_start(dst[:], src).then_inc(small_in, 16)
        load_raw(wq_raw, wqT, wq_in)
        load_chunk(0, 2)
        load_raw(wv_raw, wvT, wv_in)
        sp.dma_start(gate_u8[:], mask_rows).then_inc(gate_in, 16)
        sp.dma_start(batch_rows[:], batch_of).then_inc(gate_in, 16)
        load_chunk(0, 3)

        def store(b, h):
            sp.dma_start(attn_dram[2 * h:2 * h + 2, :, b, :].rearrange("g p q -> p g q"), o_out[:, h, :, :])\
                .then_inc(o_stored[h], 16)

        tail_w = (woT, aqT, akT, avT, aoT, f1, f2, f3)

        def load_weight(i):
            sp.dma_start(w_r[i % 4][:], tail_w[i].rearrange("(k p) n -> p k n", p=P)).then_inc(tw_in[i], 16)

        def unit(b, h, last):
            u = b * 2 + h
            if h == 1 and not last:
                load_mask(b + 1)
                load_chunk(b + 1, 0)
                load_chunk(b + 1, 1)
                load_chunk(b + 1, 2)
            if last:
                sp.wait_ge(pj_done, piece_base(u))
                load_weight(0)
                sp.wait_ge(kf_ok, 8 * 2 * B)
                sp.wait_ge(bias_ok, B)
                for k in range(KC):
                    sp.wait_ge(x_lo[k], B * 4)
                sp.wait_ge(o_stored[0], 16 * (B - 1))
                sp.wait_ge(o_stored[1], 16 * (B - 1))
                sp.dma_start(aT_r[:, :, 0:T - LQ], attn_dram[:, :, 0:B - 1, :].rearrange("k p b q -> p k (b q)"))\
                    .then_inc(at_in, 16)
                sp.wait_ge(qbd_ok, 2 * B)
                sp.dma_start(x1[:], xq.rearrange("(m p) d -> p m d", p=P)).then_inc(t_in, 16)
            if h == 1:
                wait_apart(sp, (o_ready, u))
                store(b, 0)
            if last:
                sp.wait_ge(o_stored[0], 16 * B)
                sp.dma_start(aT_r[:, 0:2, T - LQ:T], attn_dram[0:2, :, B - 1, :].rearrange("k p q -> p k q"))\
                    .then_inc(at_in, 16)
            if h == 0 and not (isinstance(b, int) and b == 0):
                wait_apart(sp, (o_ready, u))
                store(b - 1, 1)
            if h == 1 and not last:
                load_chunk(b + 1, 3)

        batches(sp, unit)
        sp.wait_ge(pj_done, piece_base(2 * B - 1) + NT)
        sp.dma_start(bo_s[:], bo.partition_broadcast(P)).then_inc(t_in, 16)
        load_weight(1)
        load_weight(2)
        load_weight(3)
        for dst, src in ((cos_s, cosT), (sin_s, sinT)):
            sp.dma_start(dst[:], src).then_inc(rot_in, 16)
        sp.wait_ge(o_ready, 2 * B)
        sp.dma_start(gw_s[:], gw).then_inc(gw_in, 16)
        sp.dma_start(fb_s[:], fb.partition_broadcast(P)).then_inc(gw_in, 16)
        computed(sp, "y1", M - 1)
        load_weight(4)
        computed(sp, "qkv", M - 1, 2)
        for i in (5, 6, 7):
            load_weight(i)
        for m in range(M):
            sp.wait_ge(res3, m + 1)
            sp.dma_start(out[m * P:(m + 1) * P, :], x1[:, m, :]).then_inc(out_done, 16)
        sp.wait_ge(out_done, 16 * M)

    @block.gpsimd
    def _(pool):
        pool.memset(ident[:], 0.0).then_inc(ident_ok, 1)
        pool.wait_ge(ident_ok, 1)
        pool.affine_select(out=ident[:], in_=ident[:], compare_op=ALU.not_equal, fill=1.0, base=0,
                           pattern=[[-1, P]], channel_multiplier=1).then_inc(ident_ok, 1)
        pool.memset(half_neg[:], -0.5).then_inc(ln_pow, 1)
        pool.memset(q_bd[:].bitcast(F32), 0.0).then_inc(qbd_zero, 1)
        def split_chunk(b, c, pieces=range(KC)):
            c0, n = CH[c]
            for k in pieces:
                pool.wait_ge(x_hi, (b * 4 + c) * KC + k + 1)
                pool.tensor_tensor(x_l[:, k, c0:c0 + n], x_raw[:, k, 0:n], x_h[:, k, c0:c0 + n].bitcast(F32),
                                   ALU.subtract).then_inc(x_lo[k], 1)

        def make_mask(b):
            wait_apart(pool, (mask_in, b * 16 + 16), (kf_ok, b * 16))
            pool.tensor_copy(mask_f[:], mask_u8[:]).then_inc(mask_ok, 1)

        def make_bias(b):
            wait_apart(pool, (sc_free, b * 32), (mask_ok, b + 1))
            pool.tensor_scalar(mask_b[:], mask_f[:], -FILL, FILL, ALU.mult, ALU.add).then_inc(bias_ok, 1)

        make_mask(0)
        make_bias(0)
        split_chunk(0, 1, (2, 3))
        pool.wait_ge(ln_pow, 1)
        for m in range(M):
            pool.wait_ge(ln_stat, 3 * m + 3)
            pool.tensor_tensor(rs0[:, m:m + 1], ve0[:, m:m + 1], half_neg[:, m:m + 1], ALU.pow).then_inc(ln_pow, 1)
        split_chunk(0, 2, (2, 3))
        split_chunk(0, 3, (2, 3))

        def unit(b, h, last):
            if h == 1 and not last:
                make_mask(b + 1)
                split_chunk(b + 1, 0, (3,))
                make_bias(b + 1)
                for c in range(1, 4):
                    split_chunk(b + 1, c)

        batches(pool, unit)

        def inv_std(n, m):
            pool.wait_ge(t_stat, n * 3 * M + 3 * m + 3)
            pool.tensor_tensor(rs1[:, m:m + 1], ve1[:, m:m + 1], half_neg[:, m:m + 1], ALU.pow).then_inc(t_pow, 1)

        def weight_lo(i, pieces=range(KC)):
            for k in pieces:
                pool.wait_ge(tw_hi, i * KC + k + 1)
                pool.tensor_tensor(w_l[i % 4][:, k, :], w_r[i % 4][:, k, :], w_h[i % 4][:, k, :].bitcast(F32),
                                   ALU.subtract).then_inc(tw_lo[i], 1)

        def cosine(m):
            for i in range(2):
                emptied(pool, "qkv", m, i)
                if m > 0:
                    pool.wait_ge(feat_ok, 4 * (m - 1) + 2 * i + 1)
                pool.tensor_tensor(rot_c[:, i, :], qk[:, i, :], cos_s[:], ALU.mult).then_inc(cos_ok, 1)

        weight_lo(1, (0, 1, 2))
        inv_std(0, 0)
        weight_lo(1, (3,))
        weight_lo(2)
        inv_std(0, 1)
        weight_lo(3, (0, 1))
        inv_std(0, 2)
        weight_lo(3, (2, 3))
        inv_std(0, 3)
        pool.wait_ge(rot_in, 32)
        cosine(0)
        pool.wait_ge(cos_ok, 2)
        pool.memset(causal[:], 0.0).then_inc(causal_ok, 1)
        for r in range(2):
            pool.wait_ge(causal_ok, 1 + r)
            pool.affine_select(out=causal[64 * r:64 * r + 64], in_=causal[64 * r:64 * r + 64], compare_op=ALU.is_ge,
                               fill=-1e9, base=0, pattern=[[-1, LQ]], channel_multiplier=1).then_inc(causal_ok, 1)
        pool.wait_ge(causal_ok, 3)
        pool.memset(pb[:], 0.0).then_inc(pb_zero, 1)
        pool.wait_ge(pb_zero, 1)
        cosine(1)
        weight_lo(4)
        cosine(2)
        cosine(3)
        weight_lo(5, (0, 1))
        inv_std(1, 0)
        weight_lo(5, (2, 3))
        inv_std(1, 1)
        weight_lo(6)
        inv_std(1, 2)
        weight_lo(7, (0, 1))
        inv_std(1, 3)
        weight_lo(7, (2, 3))

    @block.scalar
    def _(act):
        def split_chunk(b, c, pieces=range(KC)):
            c0, n = CH[c]
            for k in pieces:
                act.wait_ge(raw_in[k], (b * 4 + c) * 16 + 16)
                if not (isinstance(b, int) and b == 0):
                    act.wait_ge(pj_done, piece_base(b * 2 - 1) + V_PIECE[1][CHUNK_END[c] - 1] + 1)
                act.activation(x_h[:, k, c0:c0 + n], x_raw[:, k, 0:n], ACT.Copy).then_inc(x_hi, 1)

        def q_blocks(b, h, u, quarters=range(4)):
            if quarters[0] == 0:
                wait(act, sc_done, u * 16)
            for r in quarters:
                for par in range(2):
                    src = 32 * (r % 2) + 64 * par
                    a = act.activation(
                        q_bd[32 * r:32 * r + 32, par::2, :, 64 * (r % 2):64 * (r % 2) + 64],
                        qT[src:src + 32, :, 2 * h:2 * h + 2, bass.ds(b * LQ, LQ)].bitcast(F32)
                        .rearrange("p l g q -> p g l q"), ACT.Copy)
            if quarters[-1] == 3:
                a.then_inc(qbd_ok, 1)

        def key_hi(n):
            c, j, count = n
            c0, w_ = CH[c]
            act.wait_ge(kf_ok, count + 1)
            sl = K_SEQ.index((c, j)) % 2
            act.activation(ks[0:64, 2 * j, c0:c0 + w_], kf[0:64, sl, 0:w_], ACT.Copy).then_inc(k_hi, 1)
            act.activation(ks[64:128, 2 * j + 1, c0:c0 + w_], kf[64:128, sl, 0:w_], ACT.Copy).then_inc(k_hi, 1)

        def split_weights(dst, src, loaded):
            act.wait_ge(loaded, 16)
            for k in range(KC):
                act.activation(dst[:, k, :], src[:, k, :], ACT.Copy).then_inc(w_hi, 1)

        def first_key_hi(i):
            key_hi((*K_SEQ[i], i))

        split_chunk(0, 0)
        split_weights(wk_h, wk_raw, wk_in)
        split_chunk(0, 1)
        first_key_hi(0)
        first_key_hi(1)
        split_chunk(0, 2)
        for m in range(M):
            act.wait_ge(pro_mm, m + 1)
            act.activation(xT0[:, :, m * P:(m + 1) * P], bank[4 + m][:].rearrange("p (k t) -> p k t", k=KC), ACT.Copy)\
                .then_inc(pro_ev, 1)
        first_key_hi(2)
        first_key_hi(3)
        split_chunk(0, 3)
        first_key_hi(4)
        split_weights(wv_h, wv_raw, wv_in)
        first_key_hi(5)
        act.wait_ge(qbd_zero, 1)
        act.wait_ge(q_done, KC)
        q_blocks(0, 0, 0)
        first_key_hi(6)
        first_key_hi(7)

        def exp_pair(u, p):
            act.wait_ge(nmax_ok, u * PAIRS + p + 1)
            act.activation(prob[:, p, :], prob[:, p, :], ACT.Exp, bias=nmax[:, p:p + 1], scale=1.0,
                           accum_out=rsum[:, p:p + 1]).then_inc(exp_ok, 1)

        def out_copy(u):
            act.wait_ge(pv_done, (u + 1) * NT)
            wait(act, o_comb, u)
            for j in range(2):
                act.activation(o_sb[:, j].rearrange("p a l q -> p (a l q)"), bank[6 + j][:], ACT.Copy).then_inc(o_copy, 1)

        def out_shift(u):
            act.wait_ge(o_scale, u + 1)
            wait(act, o_ready, u)
            act.activation(o_fin[:], o_sb[64:128, :, :, 0, :], ACT.Copy).then_inc(o_shift, 1)

        def weight_hi(i, pieces=range(KC)):
            for k in pieces:
                act.wait_ge(tw_in[i], 16)
                if i >= 4:
                    act.wait_ge(tw_lo[i - 4], KC)
                act.activation(w_h[i % 4][:, k, :], w_r[i % 4][:, k, :], ACT.Copy).then_inc(tw_hi, 1)

        def attention_hi(tokens):
            act.activation(aT_h[:, :, tokens], aT_r[:, :, tokens], ACT.Copy).then_inc(at_hi, 1)

        def unit(b, h, last):
            u = b * 2 + h
            first = isinstance(b, int) and b == 0 and h == 0
            for s in range(SLOTS):
                if s < NT:
                    act.wait_ge(pj_done, piece_base(u) + (s if last else V_PIECE[h][s]) + 1)
                    prev = u * NT + s - VRING + 1 if s >= VRING else (u - 1) * NT + \
                        (s + VRING if s + VRING < NT else s) + 1
                    wait(act, pv_done, prev)
                    r = ROWS[s]
                    pj = bank[pj_bank(s if last else V_PIECE[h][s])]
                    act.activation(v[0:r, s % VRING, :, 0, :], pj[0:r, 0:256].rearrange("p (a d) -> p a d", a=PAIRS),
                                   ACT.Copy).then_inc(v_hi, 1)
                if s < 4:
                    exp_pair(u, s)
                if s in XH_SLOT and h == 1 and not last:
                    split_chunk(b + 1, XH_SLOT[s])
                if 0 <= s - T_LAG < NT:
                    t = s - T_LAG
                    r = ROWS[t]
                    act.wait_ge(t_done, u * NT + t + 1)
                    wait(act, pv_done, u * NT + t - PTRING + 1 if t >= PTRING else (u - 1) * NT +
                         last_with(NT, t, PTRING) + 1)
                    act.activation(pt[0:r, t % PTRING, :, 0, :], bank[3 + t % SC_RING][0:r, :].rearrange("p (a q) -> p a q", a=PAIRS),
                                   ACT.Copy).then_inc(t_hi, 1)
                if last and 9 <= s < 9 + KC:
                    weight_hi(0, (s - 9,))
                if last and 14 <= s < 14 + M - 1:
                    act.wait_ge(at_in, 16)
                    act.wait_ge(pj_done, piece_base(u) + NT)
                    attention_hi(slice((s - 14) * P, (s - 13) * P))
                if s in K_SLOT[h] and not last:
                    c, j = K_SLOT[h][s]
                    if (c, j) == (0, 0):
                        act.wait_ge(sc_done, (u + 1) * 16)
                    key_hi((c, j, (u + 1) * 8 + K_SEQ.index((c, j))))
                if s == 4 and not first:
                    out_copy(u - 1)
                if s == 7 and not first:
                    out_shift(u - 1)
                if s in (7, 11) and not last:
                    q_blocks(b if h == 0 else b + 1, 1 - h, u + 1, (0, 1) if s == 7 else (2, 3))

        batches(act, unit)
        weight_hi(1)
        out_copy(2 * B - 1)
        weight_hi(2, (0, 1))
        out_shift(2 * B - 1)
        weight_hi(2, (2, 3))
        act.wait_ge(at_in, 32)
        act.wait_ge(o_ready, 2 * B)
        attention_hi(slice(3 * P, T))
        weight_hi(3)

        def take(dst, kind, m, i=0, parts=KC):
            computed(act, kind, m, i)
            act.activation(dst, bank_of(kind, m, i)[:].rearrange("p (k t) -> p k t", k=parts), ACT.Copy).then_inc(ev_a, 1)

        def take_qkv(m):
            for i in range(3):
                if i < 2 and m > 0:
                    act.wait_ge(sin_ok, 2 * (m - 1) + i + 1)
                    act.wait_ge(cos_ok, 2 * (m - 1) + i + 1)
                take((qk[:, i, :] if i < 2 else v_t[:, m, :]).rearrange("p (k t) -> p k t", k=KC), "qkv", m, i)
                if m == 1 and i < 2:
                    weight_hi(4, (2 * i, 2 * i + 1))

        def high(dst, kind, m, i=0, parts=KC):
            computed(act, kind, m, i)
            act.activation(dst, bank_of(kind, m, i)[:].rearrange("p (k t) -> p k t", k=parts), ACT.Copy).then_inc(split_hi, 1)

        def take_tokens(kind, m):
            high(xT_h[:, :, m * P:(m + 1) * P], kind, m)

        def attention_tile(m):
            act.wait_ge(o_step, 2 * m + 2)
            attention_hi(slice(m * P, (m + 1) * P))

        def take_half(dst, kind, hf, banks=(0, 1)):
            for i in banks:
                high(dst[:, 2 * i:2 * i + 2, 256 * hf:256 * hf + 256], kind, hf, i, 2)

        take_tokens("t1", 0)
        take_qkv(0)
        take_tokens("t1", 1)
        for m in range(M):
            for i in range(4):
                take(featT[:, i % 2, 4 * (i // 2):4 * (i // 2) + 4, :], "feat", m, i)
            if m > 0:
                attention_tile(m - 1)
            if m == 0:
                act.wait_ge(pb_zero, 1)
            else:
                computed(act, "prob", m - 1, 3)
            for hh in range(2):
                act.wait_ge(s_sub, 2 * m + hh + 1)
                for r in range(2):
                    rr, heads = slice(64 * r, 64 * r + 64), slice(8 * hh, 8 * hh + 8)
                    act.activation(pb[rr, heads, 64 * r:64 * r + 64], sc[rr, heads, :], ACT.Exp).then_inc(s_exp, 1)
            if m < M - 1:
                take_qkv(m + 1)
            else:
                weight_hi(5)
                weight_hi(6)
            if m < M - 2:
                take_tokens("t1", m + 2)
            for i in range(4):
                take(pbT[:, 4 * i:4 * i + 4, :], "prob", m, i)
            if m == M - 1:
                take_tokens("t2", 0)
            take(o_t[:], "o", m)
            if m == M - 1:
                take_tokens("t2", 1)
        attention_tile(M - 1)
        take_half(aT_h, "f1", 0)
        weight_hi(7)
        take_tokens("t2", 2)
        take_half(xT_h, "f2", 0, (0,))
        take_tokens("t2", 3)
        take_half(xT_h, "f2", 0, (1,))
        take_half(aT_h, "f1", 1)
        take_half(xT_h, "f2", 1)
        for m in range(M):
            emptied(act, "f3", m)
            act.activation(xn[:, m, :], xn[:, m, :], ACT.Tanh).then_inc(tanh_ok, 1)

    @block.vector
    def _(dve):
        def split_chunk(b, c, pieces):
            c0, n = CH[c]
            for k in pieces:
                dve.wait_ge(x_hi, (b * 4 + c) * KC + k + 1)
                dve.tensor_tensor(x_l[:, k, c0:c0 + n], x_raw[:, k, 0:n], x_h[:, k, c0:c0 + n].bitcast(F32),
                                  ALU.subtract).then_inc(x_lo[k], 1)

        def split_weights(dst, src, high, first):
            for k in range(KC):
                dve.wait_ge(w_hi, first + k + 1)
                dve.tensor_tensor(dst[:, k, :], src[:, k, :], high[:, k, :].bitcast(F32), ALU.subtract).then_inc(w_lo, 1)

        def queries(g):
            dve.wait_ge(pro_mm, M + g + 1)
            dve.tensor_scalar(q_tmp[:], bank[4 + g][:], bq_s[:, g:g + 1], XSCALE, ALU.add, ALU.mult).then_inc(q_step, 1)
            dve.wait_ge(q_step, 2 * g + 1)
            dve.tensor_copy(qT[:, 0, g, :], q_tmp[:]).then_inc(q_step, 1)
            dve.wait_ge(q_step, 2 * g + 2)
            dve.tensor_tensor(qT[:, 1, g, :], q_tmp[:], qT[:, 0, g, :].bitcast(F32), ALU.subtract).then_inc(q_done, 1)
            dve.wait_ge(q_done, g + 1)

        def key_full(c, j, count, piece, g, bk, b):
            c0, n = CH[c]
            dve.wait_ge(pj_done, piece + 1)
            sl = K_SEQ.index((c, j)) % 2
            if K_SEQ.index((c, j)) == 0:
                dve.wait_ge(mask_ok, b + 1)
            wait(dve, k_lo, 2 * (count - 1))
            dve.scalar_tensor_tensor(kf[:, sl, 0:n], bank[bk][:, 0:n], bk_s[:, g:g + 1], mask_f[:, c0:c0 + n],
                                     ALU.add, ALU.mult).then_inc(kf_ok, 1)

        def key_lo(c, j, count):
            c0, n = CH[c]
            sl = K_SEQ.index((c, j)) % 2
            dve.wait_ge(k_hi, 2 * count + 2)
            dve.tensor_tensor(ks[64:128, 2 * j, c0:c0 + n], kf[0:64, sl, 0:n], ks[0:64, 2 * j, c0:c0 + n].bitcast(F32),
                              ALU.subtract).then_inc(k_lo, 1)
            dve.tensor_tensor(ks[0:64, 2 * j + 1, c0:c0 + n], kf[64:128, sl, 0:n],
                              ks[64:128, 2 * j + 1, c0:c0 + n].bitcast(F32), ALU.subtract).then_inc(k_lo, 1)

        def first_keys(i):
            c, j = K_SEQ[i]
            key_full(c, j, i, i, j, i % 3, 0)
            if i > 0:
                key_lo(*K_SEQ[i - 1], i - 1)

        split_chunk(0, 0, range(KC))
        split_weights(wk_l, wk_raw, wk_h, 0)
        dve.wait_ge(xq_in, 16)
        for m in range(M):
            dve.bn_stats(st0[:, m, :], xs0[:, m, :]).then_inc(ln_stat, 1)
            dve.wait_ge(ln_stat, 3 * m + 1)
            dve.bn_aggr(mv0[:, m, :], st0[:, m, :]).then_inc(ln_stat, 1)
            dve.wait_ge(ln_stat, 3 * m + 2)
            dve.tensor_scalar(ve0[:, m:m + 1], mv0[:, m, 1:2], EPS, None, ALU.add).then_inc(ln_stat, 1)
        split_chunk(0, 1, (0, 1))
        dve.wait_ge(small_in, 48)
        first_keys(0)
        first_keys(1)
        for m in range(M):
            dve.wait_ge(ln_pow, m + 2)
            dve.tensor_scalar(xs0[:, m, :], xs0[:, m, :], mv0[:, m, 0:1], rs0[:, m:m + 1],
                              ALU.subtract, ALU.mult).then_inc(ln_done, 1)
        split_chunk(0, 2, (0, 1))
        first_keys(2)
        first_keys(3)
        split_chunk(0, 3, (0, 1))
        first_keys(4)
        first_keys(5)
        split_weights(wv_l, wv_raw, wv_h, KC)
        dve.wait_ge(gate_in, 32)
        for i in range(2):
            op = dve.tensor_reduce(gate_part[:, i:i + 1], gate_u8[:], AX.X, ALU.max)
        op.then_inc(gate_ok, 1)
        for g in range(KC):
            queries(g)
        dve.wait_ge(pro_mm, M + KC + 1)
        dve.tensor_scalar(gate[:], bank[3][:, 0:2 * M:2], 1.0, None, ALU.min).then_inc(gate_ok, 1)
        first_keys(6)
        first_keys(7)

        def score_chunk(u, p, c):
            if p == 0 and c == 0:
                wait(dve, t_done, u * NT)
            c0, n = CH[c]
            n = min(n, S2 - c0)
            wait_apart(dve, (sc_done, u * 16 + 4 * p + c + 1))
            dve.tensor_tensor_reduce(prob[:, p, c0:c0 + n], bank[3 + (4 * p + c) % SC_RING][:, 0:n], mask_b[:, c0:c0 + n],
                                     1.0, -3.0e38, ALU.add, ALU.max, smax[:, p, c:c + 1]).then_inc(sc_free, 1)

        def neg_max(u, p):
            dve.wait_ge(sc_free, u * 16 + 4 * p + 4)
            dve.tensor_reduce(nmax[:, p:p + 1], smax[:, p, :], AX.X, ALU.max, negate=True).then_inc(nmax_ok, 1)

        def recip(u, h, p):
            dve.wait_ge(exp_ok, u * PAIRS + p + 1)
            if p == 0:
                wait(dve, rb_done, u - 1)
            dve.reciprocal(rinv[:, h, p:p + 1], rsum[:, p:p + 1]).then_inc(rinv_ok, 1)

        def out_add(u):
            for j in range(2):
                dve.wait_ge(o_copy, u * 2 + j + 1)
                dve.tensor_tensor(o_sb[:, j, :, 0, :], o_sb[:, j, :, 0, :], o_sb[:, j, :, 1, :], ALU.add).then_inc(o_add, 1)

        def out_scale(u):
            dve.wait_ge(o_add, (u + 1) * 2)
            dve.wait_ge(rb_done, u + 1)
            dve.tensor_tensor(o_sb[:, :, :, 0, :], o_sb[:, :, :, 0, :],
                              bank[6][:].rearrange("p (j a q) -> p j a q", j=2, a=2), ALU.mult).then_inc(o_scale, 1)

        def out_combine(u, b, h, dst):
            dve.wait_ge(o_shift, u + 1)
            dve.tensor_tensor(o_fin[:], o_sb[0:64, :, :, 0, :], o_fin[:], ALU.add).then_inc(o_comb, 1)
            dve.wait_ge(o_comb, u + 1)
            wait(dve, o_stored[h], b * 16)
            for a in range(2):
                for i in range(2):
                    for j in range(2):
                        r = 64 * a + 32 * i
                        g = 2 * h + j
                        op = dve.tensor_scalar(dst[r:r + 32, j, :], o_fin[32 * i:32 * i + 32, j, a, 64 * i:64 * i + 64],
                                               bv_s[32 * i:32 * i + 32, g, a:a + 1], None, ALU.add)
            op.then_inc(o_ready, 1)

        def value_lo(u, h, s, last):
            dve.wait_ge(v_hi, u * NT + s + 1)
            r = ROWS[s]
            pj = bank[pj_bank(s if last else V_PIECE[h][s])]
            dve.tensor_tensor(v[0:r, s % VRING, :, 1, :], pj[0:r, 0:256].rearrange("p (a d) -> p a d", a=PAIRS),
                              v[0:r, s % VRING, :, 0, :].bitcast(F32), ALU.subtract).then_inc(v_lo, 1)

        def attention_lo(n, tokens):
            dve.wait_ge(at_hi, n + 1)
            dve.tensor_tensor(aT_l[:, :, tokens], aT_r[:, :, tokens], aT_h[:, :, tokens].bitcast(F32),
                              ALU.subtract).then_inc(at_lo, 1)

        def weight_lo(i, k):
            dve.wait_ge(tw_hi, i * KC + k + 1)
            dve.tensor_tensor(w_l[i % 4][:, k, :], w_r[i % 4][:, k, :], w_h[i % 4][:, k, :].bitcast(F32),
                              ALU.subtract).then_inc(tw_lo[i], 1)

        def unit(b, h, last):
            u = b * 2 + h
            first = isinstance(b, int) and b == 0 and h == 0
            key_pending = None
            for s in range(SLOTS):
                if s < 4:
                    if s == 0 and h == 0:
                        dve.wait_ge(bias_ok, b + 1)
                    score_chunk(u, s, 0)
                    if s > 0:
                        value_lo(u, h, s - 1, last)
                    score_chunk(u, s, 1)
                    if s == 0:
                        key_lo(*K_SEQ[-1], u * 8 + 7)
                    score_chunk(u, s, 2)
                    score_chunk(u, s, 3)
                    neg_max(u, s)
                    if s > 0:
                        recip(u, h, s - 1)
                if s == 4:
                    value_lo(u, h, 3, last)
                    if h == 1 and not last:
                        split_chunk(b + 1, 0, (0, 1, 2))
                if 4 <= s < NT:
                    value_lo(u, h, s, last)
                if s == 6 and h == 0 and not first:
                    out_scale(u - 1)
                if s == 4:
                    recip(u, h, 3)
                if key_pending:
                    key_lo(*key_pending)
                    key_pending = None
                if last and 9 <= s < 9 + KC:
                    weight_lo(0, s - 9)
                if last and 14 <= s < 14 + M - 1:
                    attention_lo(s - 14, slice((s - 14) * P, (s - 13) * P))
                if s in K_SLOT[h] and not last:
                    c, j = K_SLOT[h][s]
                    nb, nh = (b, 1) if h == 0 else (b + 1, 0)
                    i = K_SEQ.index((c, j))
                    key_full(c, j, (u + 1) * 8 + i, piece_base(u) + K_PIECE[h][(c, j)], 2 * nh + j,
                             pj_bank(K_PIECE[h][(c, j)]), nb)
                    key_pending = (c, j, (u + 1) * 8 + i)
                if 0 <= s - T_LAG < NT:
                    t = s - T_LAG
                    r = ROWS[t]
                    dve.wait_ge(t_hi, u * NT + t + 1)
                    dve.tensor_tensor(pt[0:r, t % PTRING, :, 1, :], bank[3 + t % SC_RING][0:r, :].rearrange("p (a q) -> p a q", a=PAIRS),
                                      pt[0:r, t % PTRING, :, 0, :].bitcast(F32), ALU.subtract).then_inc(t_lo, 1)
                if s == 5 and not first:
                    out_add(u - 1)
                if s == 6 and h == 1 and not first:
                    out_scale(u - 1)
                if s == 8 and not first:
                    out_combine(u - 1, b - 1 if h == 0 else b, 1 - h, o_out[:, 1 - h])

        batches(dve, unit)
        dve.wait_ge(t_in, 32)
        dve.wait_ge(gate_ok, 2)

        def add_bias(m):
            dve.scalar_tensor_tensor(x1[:, m, :], bo_s[:], gate[:, m:m + 1], x1[:, m, :], ALU.mult, ALU.add).then_inc(bo_add, 1)

        add_bias(0)
        add_bias(1)
        def statistics(n, m):
            c = n * 3 * M + 3 * m
            dve.bn_stats(st1[:, m, :], x1[:, m, :]).then_inc(t_stat, 1)
            dve.wait_ge(t_stat, c + 1)
            dve.bn_aggr(mv1[:, m, :], st1[:, m, :]).then_inc(t_stat, 1)
            dve.wait_ge(t_stat, c + 2)
            dve.tensor_scalar(ve1[:, m:m + 1], mv1[:, m, 1:2], EPS, None, ALU.add).then_inc(t_stat, 1)

        def normalise(n, m):
            dve.wait_ge(t_pow, n * M + m + 1)
            if n == 1:
                computed(dve, "t1", m)
            dve.tensor_scalar(xn[:, m, :], x1[:, m, :], mv1[:, m, 0:1], rs1[:, m:m + 1],
                              ALU.subtract, ALU.mult).then_inc(t_norm, 1)

        def first_residual(m):
            computed(dve, "y1", m)
            dve.wait_ge(bo_add, m + 1)
            dve.scalar_tensor_tensor(x1[:, m, :], bank_of("y1", m)[:], gate[:, m:m + 1], x1[:, m, :], ALU.mult, ALU.add)\
                .then_inc(ev_v, 1)
            emptied(dve, "y1", m)
            statistics(0, m)

        def second_residual(m):
            computed(dve, "y2", m)
            dve.tensor_tensor(x1[:, m, :], x1[:, m, :], bank_of("y2", m)[:], ALU.add).then_inc(ev_v, 1)
            emptied(dve, "y2", m)

        def low(dst, high_, kind, m, i=0, parts=KC):
            dve.wait_ge(split_hi, SPLIT.index((kind, m, i)) + 1)
            dve.tensor_tensor(dst, bank_of(kind, m, i)[:].rearrange("p (k t) -> p k t", k=parts), high_.bitcast(F32),
                              ALU.subtract).then_inc(ev_low, 1)

        def low_tokens(kind, m):
            t_ = slice(m * P, (m + 1) * P)
            low(xT_l[:, :, t_], xT_h[:, :, t_], kind, m)

        def rotate(m, i):
            n = 2 * m + i
            emptied(dve, "qkv", m, i)
            src = qk[:, i, :].rearrange("p (h d) -> p h d", h=H)
            dst = rot_s[:, i, :].rearrange("p (h d) -> p h d", h=H)
            cs = rot_c[:, i, :].rearrange("p (h d) -> p h d", h=H)
            sn = sin_s[:].rearrange("p (h d) -> p h d", h=H)
            dve.tensor_tensor(dst[:, :, 0:16], src[:, :, 16:32], sn[:, :, 0:16], ALU.mult)
            dve.tensor_tensor(dst[:, :, 16:32], src[:, :, 0:16], sn[:, :, 16:32], ALU.mult).then_inc(sin_ok, 1)
            if m > 0:
                computed(dve, "feat", m - 1, 3)
            dve.wait_ge(sin_ok, n + 1)
            dve.wait_ge(cos_ok, n + 1)
            first = feat[:, i, :, 0, :]
            dve.tensor_tensor(first, dst, cs, ALU.add).then_inc(feat_ok, 1)
            dve.wait_ge(feat_ok, 2 * n + 1)
            dve.scalar_tensor_tensor(feat[:, i, :, 1, :], first, 0.1 if i == 0 else 1.0, first, ALU.mult, ALU.mult)\
                .then_inc(feat_ok, 1)

        def scores_less_max(m):
            for hh in range(2):
                for i in (2 * hh, 2 * hh + 1):
                    src = bank_of("score", m, i)[:].rearrange("p (a t) -> p a t", a=4)
                    h0 = 8 * hh + i % 2
                    computed(dve, "score", m, i)
                    if m > 0 and i == 0:
                        dve.wait_ge(s_exp, 4 * m)
                    for r in range(2):
                        rr = slice(64 * r, 64 * r + 64)
                        e = dve.scalar_tensor_tensor(sc[rr, h0:h0 + 7:2, :], src[rr, :, 64 * r:64 * r + 64], HD ** -0.5,
                                                     causal[rr].unsqueeze(1).to_broadcast([64, 4, LQ]), ALU.mult, ALU.add)
                    e.then_inc(ev_v, 1)
                heads = slice(8 * hh, 8 * hh + 8)
                emptied(dve, "score", m, 2 * hh + 1)
                dve.tensor_reduce(mx[:, heads], sc[:, heads, :], AX.X, ALU.max).then_inc(s_max, 1)
                dve.wait_ge(s_max, 2 * m + hh + 1)
                dve.tensor_tensor(sc[:, heads, :], sc[:, heads, :], mx[:, heads].unsqueeze(2).to_broadcast([P, 8, LQ]),
                                  ALU.subtract).then_inc(s_sub, 1)

        def inverse_sums(m):
            if m > 0:
                computed(dve, "den", m - 1)
            for r in range(2):
                rr = slice(64 * r, 64 * r + 64)
                dve.wait_ge(s_exp, 4 * m + 3 + r)
                dve.tensor_reduce(e_sum[rr], pb[rr, :, 64 * r:64 * r + 64], AX.X, ALU.add).then_inc(s_sum, 1)
            dve.wait_ge(s_sum, 4 * m + 2)
            dve.reciprocal(e_inv[:], e_sum[:]).then_inc(s_sum, 1)
            dve.wait_ge(s_sum, 4 * m + 3)
            dve.tensor_copy(e_rows[:].rearrange("p (h d) -> p h d", h=H), e_inv[:].unsqueeze(2).to_broadcast([P, H, HD]))\
                .then_inc(s_sum, 1)

        def combine_heads(m):
            computed(dve, "den", m)
            emptied(dve, "o", m)
            dve.tensor_tensor(o_t[:], o_t[:], bank_of("den", m)[:].rearrange("p (k t) -> p k t", k=KC), ALU.mult)\
                .then_inc(ev_v, 1)
            emptied(dve, "den", m)
            dve.scalar_tensor_tensor(o_q[:], o_t[:], gw_s[:, 0:1], o_t[:], ALU.mult, ALU.mult).then_inc(o_step, 1)
            dve.wait_ge(o_step, 2 * m + 1)
            dve.scalar_tensor_tensor(aT_r[:, :, m * P:(m + 1) * P], o_q[:], 0.05, o_t[:], ALU.mult, ALU.add)\
                .then_inc(o_step, 1)

        first_residual(0)
        out_add(2 * B - 1)
        out_scale(2 * B - 1)
        normalise(0, 0)
        out_combine(2 * B - 1, B - 1, 1, aT_r[:, 2:4, T - LQ:T])
        attention_lo(M - 1, slice(3 * P, T))
        first_residual(1)
        low_tokens("t1", 0)
        normalise(0, 1)
        add_bias(2)
        first_residual(2)
        add_bias(3)
        first_residual(3)
        normalise(0, 2)
        normalise(0, 3)
        dve.wait_ge(rot_in, 32)
        for i in range(2):
            rotate(0, i)
        low_tokens("t1", 1)
        dve.wait_ge(causal_ok, 3)
        dve.wait_ge(gw_in, 32)
        for m in range(M):
            if m > 0:
                attention_lo(AT_SELF + m - 1, slice((m - 1) * P, m * P))
            scores_less_max(m)
            if m == M - 1:
                second_residual(0)
                statistics(1, 0)
            inverse_sums(m)
            if m < M - 1:
                for i in range(2):
                    rotate(m + 1, i)
                if m < M - 2:
                    low_tokens("t1", m + 2)
            else:
                normalise(1, 0)
                second_residual(1)
                statistics(1, 1)
                second_residual(2)
                normalise(1, 1)
                low_tokens("t2", 0)
                low_tokens("t2", 1)
            combine_heads(m)
        attention_lo(AT_SELF + M - 1, slice((M - 1) * P, T))
        statistics(1, 2)
        normalise(1, 2)

        def low_half(dst, high_, kind, hf, banks=(0, 1)):
            for i in banks:
                g, t_ = slice(2 * i, 2 * i + 2), slice(256 * hf, 256 * hf + 256)
                low(dst[:, g, t_], high_[:, g, t_], kind, hf, i, 2)

        def before_tanh(m):
            computed(dve, "f3", m)
            dve.tensor_tensor(xn[:, m, :], bank_of("f3", m)[:], fb_s[:], ALU.add).then_inc(ev_v, 1)

        def third_residual(m):
            dve.wait_ge(tanh_ok, m + 1)
            dve.tensor_tensor(x1[:, m, :], x1[:, m, :], xn[:, m, :], ALU.add).then_inc(res3, 1)

        low_half(aT_l, aT_h, "f1", 0)
        low_tokens("t2", 2)
        second_residual(3)
        statistics(1, 3)
        normalise(1, 3)
        low_half(xT_l, xT_h, "f2", 0, (0,))
        low_tokens("t2", 3)
        low_half(xT_l, xT_h, "f2", 0, (1,))
        low_half(aT_l, aT_h, "f1", 1)
        before_tanh(0)
        low_half(xT_l, xT_h, "f2", 1)
        third_residual(0)
        for m in range(1, M):
            before_tanh(m)
            if m > 1:
                third_residual(m - 1)
        third_residual(M - 1)


    @block.tensor
    def _(pe):
        def key_piece(c, j, b, h, bk):
            c0, n = CH[c]
            g = slice((2 * h + j) * P, (2 * h + j + 1) * P)
            first = isinstance(b, int) and b == 0 and h == 0
            if h == 0 and j == 0 and not first:
                for k in range(KC):
                    pe.wait_ge(x_lo[k], b * 4 + c + 1)
            passes = [(w_, x, k) for k in range(KC) for w_, x in ((wk_h, x_h), (wk_h, x_l), (wk_l, x_h))]
            for i, (w_, x, k) in enumerate(passes):
                if first and j == 0 and i % 3 == 0:
                    pe.wait_ge(x_lo[k], c + 1)
                    if c == 0:
                        pe.wait_ge(w_lo, k + 1)
                mm_ = pe.matmul(bank[bk][:, 0:n], w_[:, k, g], x[:, k, c0:c0 + n],
                                start=(i == 0), stop=(i == len(passes) - 1))
            mm_.then_inc(pj_done, 1)

        def first_keys(i):
            wait(pe, kf_ok, i - 2)
            key_piece(*K_SEQ[i], 0, 0, i % 3)

        for i in range(4):
            first_keys(i)
        pe.wait_ge(ident_ok, 2)
        for m in range(M):
            pe.wait_ge(ln_done, m + 1)
            for k in range(KC):
                t = pe.transpose(bank[4 + m][:, k * P:(k + 1) * P], xs0[:, m, k * P:(k + 1) * P], ident[:])
            t.then_inc(pro_mm, 1)
        first_keys(4)
        first_keys(5)
        pe.wait_ge(pro_ev, M)
        pe.wait_ge(wq_in, 16)
        for g in range(KC):
            for k in range(KC):
                q = pe.matmul(bank[4 + g][:], wq_raw[:, k, g * P:(g + 1) * P], xT0[:, k, :],
                              start=(k == 0), stop=(k == KC - 1))
            q.then_inc(pro_mm, 1)
        pe.wait_ge(gate_ok, 1)
        for m in range(M):
            t = pe.matmul(bank[3][:, 2 * m:2 * m + 2], batch_rows[:, m * P:(m + 1) * P], gate_part[:], start=True, stop=True)
        t.then_inc(pro_mm, 1)
        first_keys(6)
        first_keys(7)
        pe.wait_ge(w_lo, 2 * KC)

        def bank_free(u, h, i, last):
            if i < 3:
                kind, what = PIECES[1 - h][UNIT_PIECES - 3 + i]
                if kind == "v":
                    wait(pe, v_lo, (u - 1) * NT + what + 1)
                else:
                    pe.wait_ge(kf_ok, u * 8 + K_SEQ.index(what) + 1)
            elif last:
                pe.wait_ge(v_lo, u * NT + i - 2)
            else:
                kind, what = PIECES[h][i - 3]
                if kind == "v":
                    pe.wait_ge(v_lo, u * NT + what + 1)
                else:
                    pe.wait_ge(kf_ok, (u + 1) * 8 + K_SEQ.index(what) + 1)

        def score_chunk(u, p, c):
            if p == 0 and c == 0:
                pe.wait_ge(qbd_ok, u + 1)
                if isinstance(u, int) and u == 0:
                    pe.wait_ge(gate_ok, 2)
            c0, n = CH[c]
            i = 4 * p + c
            pe.wait_ge(k_lo, u * 16 + 2 * (2 * c + p // 2 + 1))
            if i < SC_RING:
                wait(pe, t_lo, (u - 1) * NT + last_with(NT, i, SC_RING) + 1)
            else:
                pe.wait_ge(sc_free, u * 16 + i - SC_RING + 1)
            for l in range(2):
                s_ = pe.matmul(bank[3 + i % SC_RING][:, 0:n], q_bd[:, p, 1 - l, :], ks[:, p, c0:c0 + n],
                               start=(l == 0), stop=(l == 1))
            s_.then_inc(sc_done, 1)

        def value_tile(u, h, s, last, parts=((0, 12),)):
            i = s if last else V_PIECE[h][s]
            bank_free(u, h, i, last)
            r = ROWS[s]
            t0 = s * P
            passes = [(x, w_, k) for k in range(KC) for x, w_ in ((x_h, wv_h), (x_h, wv_l), (x_l, wv_h))]
            for a, z in parts:
                for n in range(a, z):
                    x, w_, k = passes[n]
                    v_ = pe.matmul(bank[pj_bank(i)][0:r, 0:256], x[:, k, t0:t0 + r], w_[:, k, 256 * h:256 * h + 256],
                                   start=(n == 0), stop=(n == len(passes) - 1))
                if z == len(passes):
                    v_.then_inc(pj_done, 1)
                yield

        def turn_tile(u, t):
            r = ROWS[t]
            if t == 0:
                pe.wait_ge(exp_ok, (u + 1) * PAIRS)
            if t >= SC_RING:
                pe.wait_ge(t_lo, u * NT + t - SC_RING + 1)
            else:
                pe.wait_ge(sc_free, u * 16 + last_with(16, t, SC_RING) + 1)
            for p in range(PAIRS):
                t_ = pe.transpose(bank[3 + t % SC_RING][0:r, p * P:(p + 1) * P], prob[:, p, t * P:t * P + r], ident[:])
            t_.then_inc(t_done, 1)

        def product_tile(u, t):
            r = ROWS[t]
            if t == 0:
                wait(pe, o_scale, u)
            pe.wait_ge(v_lo, u * NT + t + 1)
            pe.wait_ge(t_lo, u * NT + t + 1)
            for p in range(PAIRS):
                o_ = pe.matmul(bank[6 + p // 2][:, 256 * (p % 2):256 * (p % 2) + 256], v[0:r, t % VRING, p, :, :],
                               pt[0:r, t % PTRING, p, :, :], start=(t == 0 and p % 2 == 0), stop=(t == NT - 1),
                               skip_group_check=True)
            o_.then_inc(pv_done, 1)

        def spread_scales(u, h):
            wait(pe, o_copy, u * 2 + 1)
            pe.wait_ge(rinv_ok, (u + 1) * PAIRS)
            for p in range(PAIRS):
                r_ = pe.matmul(bank[6][:, p * P:(p + 1) * P], rinv[:, h, p:p + 1].to_broadcast([P, P]), ident[:],
                               start=True, stop=True)
            r_.then_inc(rb_done, 1)

        def begin(kind, m, i=0):
            n = job(kind, m, i)
            if n >= 8:
                emptied(pe, *JOBS[n - 8])
            return bank[n % 8]

        def weight_ready(i):
            pe.wait_ge(tw_lo[i], KC)

        def passes(stationary, moving):
            return [(stationary[a], moving[b], k) for k in range(KC) for a, b in ((0, 0), (0, 1), (1, 0))]

        def rows_product(xt, i, kind, m, n=0):
            bk = begin(kind, m, n)
            steps = passes(xt, (w_h[i % 4], w_l[i % 4]))
            for z, (x_, w_, k) in enumerate(steps):
                q = pe.matmul(bk[:], x_[:, k, m * P:(m + 1) * P], w_[:, k, :], start=(z == 0), stop=(z == len(steps) - 1))
            q.then_inc(mm, 1)

        def first_output(m):
            pe.wait_ge(at_lo, m + 1)
            rows_product((aT_h, aT_l), 0, "y1", m)

        def unit(b, h, last):
            u = b * 2 + h
            for s in range(SLOTS):
                if s < 4:
                    value = value_tile(u, h, s, last, ((0, 6), (6, 9), (9, 12)))
                    score_chunk(u, s, 0)
                    score_chunk(u, s, 1)
                    next(value)
                    score_chunk(u, s, 2)
                    next(value)
                    score_chunk(u, s, 3)
                    next(value)
                elif s < NT:
                    next(value_tile(u, h, s, last))
                if s in K_SLOT[h] and not last:
                    c, j = K_SLOT[h][s]
                    i = K_PIECE[h][(c, j)]
                    bank_free(u, h, i, last)
                    key_piece(c, j, b if h == 0 else b + 1, 1 - h, pj_bank(i))
                if 0 <= s - T_LAG < NT:
                    turn_tile(u, s - T_LAG)
                if last and s == SLOTS - 3:
                    pe.wait_ge(v_lo, 2 * B * NT)
                    weight_ready(0)
                    first_output(0)
                if 0 <= s - PV_LAG < NT:
                    product_tile(u, s - PV_LAG)
                if s == 5 + h and not (isinstance(b, int) and b == 0 and h == 0):
                    spread_scales(u - 1, 1 - h)

        batches(pe, unit)

        def cols_product(i, xt, kind, hf, banks=(0, 1)):
            steps = passes((w_h[i % 4], w_l[i % 4]), xt)
            for n in banks:
                bk = begin(kind, hf, n)
                for a in range(2):
                    g = 2 * n + a
                    for z, (w_, x_, k) in enumerate(steps):
                        q = pe.matmul(bk[:, 256 * a:256 * a + 256], w_[:, k, g * P:(g + 1) * P],
                                      x_[:, k, 256 * hf:256 * hf + 256], start=(z == 0), stop=(z == len(steps) - 1))
                q.then_inc(mm, 1)

        def turn4(src, kind, m, i=0):
            bk = begin(kind, m, i)
            for a in range(4):
                t_ = pe.transpose(bk[:, a * P:(a + 1) * P], src(a), ident[:])
            t_.then_inc(mm, 1)

        def turn_tokens(kind, m):
            pe.wait_ge(t_norm, m + 1 + (M if kind == "t2" else 0))
            turn4(lambda a: xn[:, m, a * P:(a + 1) * P], kind, m)

        def project(m):
            emptied(pe, "t1", m)
            for i in range(3):
                if m == 0:
                    weight_ready(1 + i)
                rows_product(xT, 1 + i, "qkv", m, i)

        def scores(m):
            for i in range(4):
                f, q4 = i % 2, i // 2
                if q4 == 0:
                    pe.wait_ge(feat_ok, 4 * m + 2 * f + 2)
                flat = feat[:, f].rearrange("p h s d -> p (h s d)")
                turn4(lambda a: flat[:, (4 * q4 + a) * P:(4 * q4 + a + 1) * P], "feat", m, i)
            for i in range(4):
                if i % 2 == 0:
                    emptied(pe, "feat", m, i + 1)
                bk = begin("score", m, i)
                r = 64 * (i % 2)
                for a in range(4):
                    hp = 4 * (i // 2) + a
                    s_ = pe.matmul(bk[:, a * P:(a + 1) * P], featT[r:r + 64, 0, hp, :], featT[r:r + 64, 1, hp, :],
                                   start=True, stop=True)
                s_.then_inc(mm, 1)

        def turn_probabilities(m):
            for i in range(4):
                pe.wait_ge(s_exp, 4 * m + 2 * (i // 2) + 2)
                turn4(lambda a: pb[:, 4 * i + a, :], "prob", m, i)

        def attend(m):
            bk = begin("o", m)
            for hd in range(H):
                if hd % 4 == 0:
                    emptied(pe, "prob", m, hd // 4)
                r = 32 * (hd % 4)
                o_ = pe.matmul(bk[r:r + 32, (hd // 4) * P:(hd // 4 + 1) * P], v_t[:, m, HD * hd:HD * hd + HD], pbT[:, hd, :],
                               start=True, stop=True)
            o_.then_inc(mm, 1)
            bk = begin("den", m)
            pe.wait_ge(s_sum, 4 * m + 4)
            for g in range(4):
                o_ = pe.matmul(bk[:, g * P:(g + 1) * P], e_rows[:, g * P:(g + 1) * P],
                               ident[:], start=True, stop=True)
            o_.then_inc(mm, 1)

        aT, xT = (aT_h, aT_l), (xT_h, xT_l)
        pe.wait_ge(t_lo, 2 * B * NT)

        def second_output(m):
            pe.wait_ge(at_lo, AT_SELF + m + 1)
            rows_product(aT, 4, "y2", m)

        spread_scales(2 * B - 1, 1)
        first_output(1)
        first_output(2)
        turn_tokens("t1", 0)
        pe.wait_ge(o_scale, 2 * B)
        first_output(3)
        project(0)
        turn_tokens("t1", 1)
        for m in range(M - 1):
            scores(m)
            project(m + 1)
            if m < M - 2:
                turn_tokens("t1", m + 2)
            turn_probabilities(m)
            attend(m)
        scores(3)
        weight_ready(4)
        for m in range(M - 1):
            second_output(m)
        turn_probabilities(3)
        turn_tokens("t2", 0)
        attend(3)
        turn_tokens("t2", 1)
        weight_ready(5)
        emptied(pe, "t2", 1)
        cols_product(5, xT, "f1", 0)
        turn_tokens("t2", 2)
        second_output(3)
        weight_ready(6)
        emptied(pe, "f1", 0, 1)
        cols_product(6, aT, "f2", 0, (0,))
        turn_tokens("t2", 3)
        cols_product(6, aT, "f2", 0, (1,))
        emptied(pe, "t2", 3)
        cols_product(5, xT, "f1", 1)
        weight_ready(7)

        def last_product(m):
            emptied(pe, "f2", m // 2, 1)
            rows_product(xT, 7, "f3", m)

        last_product(0)
        emptied(pe, "f1", 1, 1)
        cols_product(6, aT, "f2", 1)
        for m in range(1, M):
            last_product(m)

    base.close()
    return nc


def kernel(x, ctx_1024, mask_BxS2_bk1, L0_xattn_Wq, L0_xattn_bq, L0_xattn_Wk, L0_xattn_bk, L0_xattn_Wv, L0_xattn_bv,
           L0_xattn_Wo, L0_xattn_bo, L0_attn_Wq, L0_attn_Wk, L0_attn_Wv, L0_attn_Wo, L0_attn_gate_w, L0_ffn_weight,
           L0_ffn_aux_weight1, L0_ffn_aux_weight2, L0_ffn_bias):
    import concourse.bacc as bacc
    from concourse.bass_utils import run_bass_kernel_spmd

    def tr(a):
        return np.ascontiguousarray(np.asarray(a).T)

    def cols(a):
        return np.ascontiguousarray(np.asarray(a).reshape(KC, P).T)

    ctx = np.asarray(ctx_1024)
    ctxT = np.zeros((B, D, S2P), ctx.dtype)
    ctxT[:, :, :S2] = ctx.transpose(0, 2, 1)
    mask = np.zeros((B, S2P), bool)
    mask[:, :S2] = np.asarray(mask_BxS2_bk1)

    parts = P // B
    mask_rows = np.zeros((B, parts * GC), bool)
    mask_rows[:, :S2] = mask[:, :S2]
    mask_rows = mask_rows.reshape(P, GC)
    batch_of = np.repeat(np.repeat(np.eye(B, dtype=np.float32), parts, 0), LQ, 1)

    half = HD // 2
    inv = (1.0 / np.float32(10000.0) ** (np.arange(half, dtype=np.float32) / np.float32(half))).astype(np.float32)
    ang = (np.arange(LQ, dtype=np.float32)[:, None] * inv[None, :]).astype(np.float32)
    cos, sin = np.cos(ang).astype(np.float32), np.sin(ang).astype(np.float32)
    cosT = np.ascontiguousarray(np.tile(np.concatenate([cos, cos], 1), (P // LQ, H)))
    sinT = np.ascontiguousarray(np.tile(np.concatenate([-sin, sin], 1), (P // LQ, H)))

    arrays = {
        "xq": np.ascontiguousarray(np.asarray(x).reshape(T, D)), "ctxT": ctxT, "mask": mask,
        "wqT": tr(L0_xattn_Wq), "wkT": tr(L0_xattn_Wk), "wvT": tr(L0_xattn_Wv), "woT": tr(L0_xattn_Wo),
        "bq": cols(L0_xattn_bq), "bk": cols(L0_xattn_bk),
        "bv": np.ascontiguousarray(np.asarray(L0_xattn_bv).reshape(KC, 2, 64).transpose(2, 0, 1)),
        "bo": np.asarray(L0_xattn_bo),
        "aqT": tr(L0_attn_Wq), "akT": tr(L0_attn_Wk), "avT": tr(L0_attn_Wv), "aoT": tr(L0_attn_Wo),
        "gw": np.ascontiguousarray(np.tile(np.asarray(L0_attn_gate_w), P // HD).reshape(P, 1)),
        "f1": np.asarray(L0_ffn_weight), "f2": np.asarray(L0_ffn_aux_weight1), "f3": np.asarray(L0_ffn_aux_weight2),
        "fb": np.asarray(L0_ffn_bias), "cosT": cosT, "sinT": sinT, "mask_rows": mask_rows, "batch_of": batch_of,
    }
    nc = bacc.Bacc("TRN2", target_bir_lowering=False, num_devices=1)
    args = [nc.dram_tensor(n, a.shape, mybir.dt.from_np(a.dtype), kind="ExternalInput").ap() for n, a in arrays.items()]
    out = nc.dram_tensor("out", (T, D), F32, kind="ExternalOutput").ap()
    build(nc, *args, out)
    r = run_bass_kernel_spmd(nc, [arrays], core_ids=[0])
    return r.results[0]["out"].reshape(B, LQ, D)
```
